# Optimizing a Trainium2 kernel written in Bass

```python
import numpy as np
import jax
import jax.numpy as jnp

def _softmax(x, axis=-1):
    return jax.nn.softmax(x, axis=axis)

def _gelu(x):
    return jax.nn.gelu(x, approximate=True)

def _silu(x):
    return jax.nn.silu(x)

def _sigmoid(x):
    return jax.nn.sigmoid(x)

def _layernorm(x, axis=-1, eps=1e-05):
    m = jnp.mean(x, axis=axis, keepdims=True)
    v = jnp.var(x, axis=axis, keepdims=True)
    return (x - m) / jnp.sqrt(v + eps)

def _scatter_add(tgt, idx, src, axis=0):
    return tgt.at[idx].add(src)

def _segment_sum(src, seg, n):
    return jax.ops.segment_sum(src, seg, n)
kernel_name = 'mk_prb_d1_jaxref_r8_c76fae'

def setup_inputs(seed: int=0):
    np.random.seed(seed)
    _w = jnp.asarray

    def _L0_attn_setup():
        import jax, jax.numpy as jnp
        import numpy as np
        B, S, D = (4, 512, 128)
        DK, DV = (128, 128)
        key = jax.random.key(seed)
        ks = jax.random.split(key, 7)
        s = 1.0 / np.sqrt(D)
        return {'x': jax.random.normal(ks[0], (B, S, D), dtype=jnp.float32), 'Wq': jax.random.uniform(ks[1], (D, DK), dtype=jnp.float32, minval=-s, maxval=s), 'bq': jax.random.uniform(ks[2], (DK,), dtype=jnp.float32, minval=-s, maxval=s), 'Wk': jax.random.uniform(ks[3], (D, DK), dtype=jnp.float32, minval=-s, maxval=s), 'bk': jax.random.uniform(ks[4], (DK,), dtype=jnp.float32, minval=-s, maxval=s), 'Wv': jax.random.uniform(ks[5], (D, DV), dtype=jnp.float32, minval=-s, maxval=s), 'bv': jax.random.uniform(ks[6], (DV,), dtype=jnp.float32, minval=-s, maxval=s)}
    _L0_attn_in = _L0_attn_setup()

    def _L0_ffn_setup():
        import jax, jax.numpy as jnp
        import numpy as np
        HIDDEN_SIZE = 128
        NUM_EXPERTS = 8
        MOE_INTERMEDIATE_SIZE = 176
        NUM_EXPERTS_PER_TOK = 2
        SHARED_EXPERT_INTERMEDIATE_SIZE = 352
        B, T = (2, 128)
        W_SCALE = 0.02
        key = jax.random.key(seed)
        ks = jax.random.split(key, 8)
        H, E, I, SI = (HIDDEN_SIZE, NUM_EXPERTS, MOE_INTERMEDIATE_SIZE, SHARED_EXPERT_INTERMEDIATE_SIZE)
        return {'x': jax.random.normal(ks[0], (B, T, H), jnp.float32), 'gate_w': jax.random.normal(ks[1], (E, H), jnp.float32) * W_SCALE, 'experts_gate_up': jax.random.normal(ks[2], (E, 2 * I, H), jnp.float32) * W_SCALE, 'experts_down': jax.random.normal(ks[3], (E, H, I), jnp.float32) * W_SCALE, 'shared_gate_w': jax.random.normal(ks[4], (SI, H), jnp.float32) * W_SCALE, 'shared_up_w': jax.random.normal(ks[5], (SI, H), jnp.float32) * W_SCALE, 'shared_down_w': jax.random.normal(ks[6], (H, SI), jnp.float32) * W_SCALE, 'shared_expert_gate_w': jax.random.normal(ks[7], (1, H), jnp.float32) * W_SCALE}
    _L0_ffn_in = _L0_ffn_setup()
    _d = {'L0_attn_x': _L0_attn_in['x'], 'L0_attn_Wq': _L0_attn_in['Wq'], 'L0_attn_bq': _L0_attn_in['bq'], 'L0_attn_Wk': _L0_attn_in['Wk'], 'L0_attn_bk': _L0_attn_in['bk'], 'L0_attn_Wv': _L0_attn_in['Wv'], 'L0_attn_bv': _L0_attn_in['bv'], 'L0_ffn_gate_w': _L0_ffn_in['gate_w'], 'L0_ffn_experts_gate_up': _L0_ffn_in['experts_gate_up'], 'L0_ffn_experts_down': _L0_ffn_in['experts_down'], 'L0_ffn_shared_gate_w': _L0_ffn_in['shared_gate_w'], 'L0_ffn_shared_up_w': _L0_ffn_in['shared_up_w'], 'L0_ffn_shared_down_w': _L0_ffn_in['shared_down_w'], 'L0_ffn_shared_expert_gate_w': _L0_ffn_in['shared_expert_gate_w']}
    _x0 = _d['L0_attn_x']
    _d['L0_attn_x'] = jax.random.normal(jax.random.fold_in(jax.random.key(seed), 1), (8, 512, 128), dtype=_x0.dtype)
    del _x0
    return _d

def reference(L0_attn_x, L0_attn_Wq, L0_attn_bq, L0_attn_Wk, L0_attn_bk, L0_attn_Wv, L0_attn_bv, L0_ffn_gate_w, L0_ffn_experts_gate_up, L0_ffn_experts_down, L0_ffn_shared_gate_w, L0_ffn_shared_up_w, L0_ffn_shared_down_w, L0_ffn_shared_expert_gate_w):

    def _L0_attn_ref(x, Wq, bq, Wk, bk, Wv, bv):
        import jax, jax.numpy as jnp
        import numpy as np
        B, S, D = (4, 512, 128)
        DK, DV = (128, 128)
        Q = jnp.einsum('bsd,dk->bsk', x, Wq) + bq
        K = jnp.einsum('bsd,dk->bsk', x, Wk) + bk
        V = jnp.einsum('bsd,dv->bsv', x, Wv) + bv
        scale = 1.0 / np.sqrt(DK)
        scores = jnp.einsum('bqk,bsk->bqs', Q, K) * scale
        attn = jax.nn.softmax(scores, axis=-1)
        return jnp.einsum('bqs,bsv->bqv', attn, V)

    def _L0_ffn_ref(x, gate_w, experts_gate_up, experts_down, shared_gate_w, shared_up_w, shared_down_w, shared_expert_gate_w):
        import jax, jax.numpy as jnp
        import numpy as np
        HIDDEN_SIZE = 128
        NUM_EXPERTS = 8
        MOE_INTERMEDIATE_SIZE = 176
        NUM_EXPERTS_PER_TOK = 2
        SHARED_EXPERT_INTERMEDIATE_SIZE = 352
        B, T = (2, 128)
        W_SCALE = 0.02
        Bx, Tx, H = x.shape
        E = gate_w.shape[0]
        I = experts_down.shape[2]
        x_flat = x.reshape(Bx * Tx, H)
        logits = x_flat @ gate_w.T
        scores = jax.nn.softmax(logits, axis=-1)
        _, topk_ids = jax.lax.top_k(scores, NUM_EXPERTS_PER_TOK)
        in_topk = jax.nn.one_hot(topk_ids, E, dtype=x.dtype).sum(axis=1)
        w = scores * in_topk
        gu = jnp.einsum('nh,eih->nei', x_flat, experts_gate_up)
        g, u = (gu[..., :I], gu[..., I:])
        h = jax.nn.silu(g) * u
        expert_out = jnp.einsum('nei,ehi->neh', h, experts_down)
        out = jnp.einsum('neh,ne->nh', expert_out, w)
        shared = jax.nn.silu(x_flat @ shared_gate_w.T) * (x_flat @ shared_up_w.T) @ shared_down_w.T
        shared_weight = jax.nn.sigmoid(x_flat @ shared_expert_gate_w.T)
        out = out + shared_weight * shared
        return out.reshape(Bx, Tx, H)
    x = L0_attn_x
    xn = _layernorm(x, axis=-1)
    x = x + _L0_attn_ref(xn, L0_attn_Wq, L0_attn_bq, L0_attn_Wk, L0_attn_bk, L0_attn_Wv, L0_attn_bv) + _L0_ffn_ref(xn, L0_ffn_gate_w, L0_ffn_experts_gate_up, L0_ffn_experts_down, L0_ffn_shared_gate_w, L0_ffn_shared_up_w, L0_ffn_shared_down_w, L0_ffn_shared_expert_gate_w)
    return x

_drawn_inputs = setup_inputs


def setup_inputs(seed=0):
    import zlib

    import numpy as np

    out = dict(_drawn_inputs(seed))
    spreads = {}
    factors = {'L0_attn_Wq': 2.95,
     'L0_attn_bq': 22.166,
     'L0_attn_Wk': 2.933,
     'L0_attn_bk': 64.0,
     'L0_ffn_gate_w': 8.0,
     'L0_ffn_experts_gate_up': 8.0,
     'L0_ffn_experts_down': 8.0,
     'L0_ffn_shared_gate_w': 8.0,
     'L0_ffn_shared_up_w': 8.0,
     'L0_ffn_shared_down_w': 8.0,
     'L0_ffn_shared_expert_gate_w': 8.0,
     'L0_attn_bv': 5.167}
    for name, (base, spread) in spreads.items():
        noise = np.random.default_rng([zlib.crc32(name.encode()), seed]).standard_normal(out[name].shape)
        drawn = base * np.exp(spread * noise) if base else spread * noise
        out[name] = jnp.asarray(drawn.astype(out[name].dtype))
    for name, factor in factors.items():
        out[name] = (out[name] * factor).astype(out[name].dtype)
    return out
```

```python
from contextlib import ExitStack

import concourse.bass as bass
from concourse import mybir

F32 = mybir.dt.float32
F32R = mybir.dt.float32r
ALU = mybir.AluOpType
ACT = mybir.ActivationFunctionType
AX = mybir.AxisListType

P = 128
B, S, D = 8, 512, 128
TJ = S // P
E, I, SI = 8, 176, 352
K_TOP = 2
R = E + 1
HID = E * I + SI
NT = -(-HID // P)
ROWS = [min(P, HID - P * t) for t in range(NT)]
CH = 4
CW = HID // CH
VG = D + R + 1
SCALE = 1.0 / float(D) ** 0.5
EPS = 1e-5
WB_LAG, DOWN_LAG = 3, 5
RING = 4
GATE_STEPS = 12


def moe_attention_layer(nc, x, w_qkvr, biases, w_up, w_down, consts, select, out):
    x_v = x.rearrange("b (p j) d -> b p (j d)", j=TJ)
    out_v = out.rearrange("b (p j) d -> b p (j d)", j=TJ)

    with ExitStack() as ctx:
        def sb(name, shape, dt=F32):
            return ctx.enter_context(nc.sbuf_tensor(name, shape, dt))

        def pb(name, shape):
            return ctx.enter_context(nc.psum_tensor(name, shape, F32))

        def sem(name):
            return ctx.enter_context(nc.semaphore(name))

        wq_raw = sb("wq_raw", [P, 2 * D + VG])
        wqs = sb("wqs", [P, D])
        bias = sb("bias", [P, 3])
        bqs = sb("bqs", [P, 1])
        wup_raw = sb("wup_raw", [P, CH, 2 * CW])
        wdn_raw = sb("wdn_raw", [P, NT * D])
        cst = sb("cst", [P, P + E * E])
        sel_raw = sb("sel_raw", [2 * R, NT * P])
        wq_hi, wq_lo = sb("wq_hi", [P, 2 * D + VG], F32R), sb("wq_lo", [P, 2 * D + VG], F32R)
        wup_hi, wup_lo = sb("wup_hi", [P, CH, 2 * CW], F32R), sb("wup_lo", [P, CH, 2 * CW], F32R)
        wdn_hi, wdn_lo = sb("wdn_hi", [P, NT * D], F32R), sb("wdn_lo", [P, NT * D], F32R)
        sel = sb("sel", [2 * R, NT * P], F32R)
        ident = cst[:, 0:P]
        tie = cst[:, P:P + E * E]
        mhalf = sb("mhalf", [P, TJ])

        xs = sb("xs", [P, 2, S])
        stats = sb("stats", [P, TJ, 6])
        mv = sb("mv", [P, TJ, 2])
        veps = sb("veps", [P, TJ])
        rstd = sb("rstd", [P, TJ])
        xn = sb("xn", [P, S])
        xT_hi, xT_lo = sb("xT_hi", [P, 2, S], F32R), sb("xT_lo", [P, 2, S], F32R)
        kT_hi, kT_lo = sb("kT_hi", [P, S], F32R), sb("kT_lo", [P, S], F32R)
        qT_hi, qT_lo = sb("qT_hi", [P, S], F32R), sb("qT_lo", [P, S], F32R)
        v_hi, v_lo = sb("v_hi", [P, TJ, D], F32R), sb("v_lo", [P, TJ, D], F32R)
        probs = sb("probs", [P, TJ, S])
        nmax = sb("nmax", [P, TJ])
        psums = sb("psums", [P, TJ])
        pinv = sb("pinv", [P, TJ])
        pT_hi, pT_lo = sb("pT_hi", [P, TJ, S], F32R), sb("pT_lo", [P, TJ, S], F32R)
        logit = sb("logit", [P, TJ, R])
        diff = sb("diff", [P, TJ, E, E])
        beats = sb("beats", [P, TJ, E, E])
        rank = sb("rank", [P, TJ, E])
        lmax = sb("lmax", [P, TJ])
        ein = sb("ein", [P, TJ, R])
        eout = sb("eout", [P, TJ, R])
        den = sb("den", [P, TJ, 2])
        rden = sb("rden", [P, TJ, 2])
        wtop = sb("wtop", [P, TJ, E])
        wts = sb("wts", [P, TJ, R])
        wsplit = sb("wsplit", [P, TJ, 2 * R], F32R)
        wT = sb("wT", [2 * R, S], F32R)
        silu = sb("silu", [P, 2, S])
        prod = sb("prod", [P, RING, S])
        hid = sb("hid", [P, 2, S])
        h_hi, h_lo = sb("h_hi", [P, RING, S], F32R), sb("h_lo", [P, RING, S], F32R)
        accT = sb("accT", [P, S])
        res = sb("res", [P, S])

        att = pb("att", [P, 2, S])
        gu = pb("gu", [P, 4, S])
        wrow = pb("wrow", [P, S])
        acc = pb("acc", [P, S])

        s_wq, s_cst, s_dn, s_sel, s_store = map(
            sem, ["qkv_loaded", "consts_loaded", "down_loaded", "select_loaded", "stored"])
        s_x = [sem("x_even_loaded"), sem("x_odd_loaded")]
        s_up = [sem(f"up_loaded{c}") for c in range(CH)]
        s_wqs, s_mhalf = sem("q_scaled"), sem("mhalf_set")
        s_wqhi, s_wqlo = sem("qkv_hi"), sem("qkv_lo")
        s_uphi, s_uplo, s_uplo_v = sem("up_hi"), sem("gate_lo"), sem("up_lo")
        s_dnhi, s_dnlo, s_selr = sem("down_hi"), sem("down_lo"), sem("select_rounded")
        s_xt, s_k, s_q, s_v, s_sc, s_pt, s_av, s_wt, s_ot = map(
            sem, ["xT_made", "k_made", "q_made", "v_made", "scores_made", "pT_made", "av_made",
                  "wT_made", "outT_turned"])
        s_g, s_u, s_wb, s_d = map(sem, ["gate_made", "up_made", "wrow_made", "down_made"])
        s_gexp, s_exp, s_silu, s_xhi, s_khi, s_qhi, s_vhi, s_wts, s_pthi, s_accs, s_hhi = map(
            sem, ["router_exp", "probs_exp", "silu_made", "xT_hi_made", "k_hi_made", "q_hi_made",
                  "v_hi_made", "wT_kept", "pT_hi_made", "acc_kept", "h_hi_made"])
        s_st, s_mv, s_ve, s_xn, s_xlo, s_klo, s_qlo, s_vlo, s_gate, s_max, s_pinv, s_pn, s_ptlo, \
            s_b, s_c, s_out = map(
                sem, ["stats_made", "moments_made", "var_eps", "xn_made", "xT_lo_made", "k_lo_made",
                      "q_lo_made", "v_lo_made", "router_step", "max_made", "sum_inverted",
                      "probs_scaled", "pT_lo_made", "prod_made", "hid_made", "result_made"])
        s_split = sem("weights_hi")
        s_rstd, s_hlo = sem("rstd_made"), sem("h_lo_made")

        def tile(b, t):
            return b * NT + t

        def ring(par, t, size):
            return (NT * par + t) % size

        def bodies(eng, body):
            body(0, 0, 0, True, False)
            with eng.Fori(0, (B - 2) // 2) as i:
                body(i * 2 + 1, 1, i + 1, False, False)
                body(i * 2 + 2, 0, i + 1, False, False)
            body(B - 1, (B - 1) % 2, B // 2, False, True)

        block = ctx.enter_context(nc.Block())

        @block.sync
        def _(sp):
            sp.dma_start(xs[:, 0, :], x_v[0]).then_inc(s_x[0], 16)
            sp.dma_start(cst[:], consts).then_inc(s_cst, 16)
            sp.dma_start(wq_raw[:], w_qkvr).then_inc(s_wq, 16)
            sp.dma_start(bias[:], biases).then_inc(s_wq, 16)
            sp.dma_start(wup_raw[:, 0], w_up[:, 0]).then_inc(s_up[0], 16)
            sp.dma_start(sel_raw[:], select).then_inc(s_sel, 16)
            for c in range(1, CH):
                sp.dma_start(wup_raw[:, c], w_up[:, c]).then_inc(s_up[c], 16)
            sp.dma_start(wdn_raw[:], w_down).then_inc(s_dn, 16)
            sp.dma_start(xs[:, 1, :], x_v[1]).then_inc(s_x[1], 16)

            sp.sem_inc(s_store, 16)

            def store(b):
                sp.wait_ge(s_out, b + 1)
                sp.dma_start(out_v[b] if isinstance(b, int) else out_v[bass.ds(b, 1)].rearrange("a p n -> (a p) n"),
                             res[:]).then_inc(s_store, 16)

            def load(b, par):
                sp.dma_start(xs[:, par, :],
                             x_v[b] if isinstance(b, int) else x_v[bass.ds(b, 1)].rearrange("a p n -> (a p) n")).then_inc(s_x[par], 16)

            with sp.Fori(0, (B - 2) // 2) as i:
                for half in range(2):
                    store(i * 2 + half)
                    load(i * 2 + half + 2, half)
            store(B - 2)
            store(B - 1)
            sp.wait_ge(s_store, 16 * (B + 1))

        @block.gpsimd
        def _(pool):
            nc.gpsimd.memset(mhalf[:], -0.5).then_inc(s_mhalf, 1)

            def norm(b):
                pool.wait_ge(s_ve, b + 1)
                if isinstance(b, int) and b == 0:
                    pool.wait_ge(s_mhalf, 1)
                nc.gpsimd.tensor_tensor(rstd[:], veps[:], mhalf[:], ALU.pow).then_inc(s_rstd, 1)

            norm(0)
            for c in range(CH):
                pool.wait_ge(s_uphi, c + 1)
                nc.gpsimd.tensor_tensor(wup_lo[:, c, 0:CW], wup_raw[:, c, 0:CW],
                                        wup_hi[:, c, 0:CW].bitcast(F32), ALU.subtract).then_inc(s_uplo, 1)
            for c in range(2):
                w = NT * D // 2
                pool.wait_ge(s_dnhi, c + 1)
                nc.gpsimd.tensor_tensor(wdn_lo[:, c * w:(c + 1) * w], wdn_raw[:, c * w:(c + 1) * w],
                                        wdn_hi[:, c * w:(c + 1) * w].bitcast(F32), ALU.subtract).then_inc(s_dnlo, 1)

            def hidden_lo(b, par, t):
                M = ROWS[t % NT]
                pool.wait_ge(s_hhi, tile(b, t) + 1)
                nc.gpsimd.tensor_tensor(h_lo[0:M, ring(par, t, RING)], hid[0:M, ring(par, t, 2)],
                                        h_hi[0:M, ring(par, t, RING)].bitcast(F32), ALU.subtract).then_inc(s_hlo, 1)

            def body(b, par, pair, first, last):
                for t in range(NT):
                    if not first or t >= WB_LAG:
                        hidden_lo(b, par, t - WB_LAG)
                    if t == 9 and not last:
                        norm(b + 1)

            bodies(pool, body)
            for t in range(NT, NT + WB_LAG):
                hidden_lo(B - 1, (B - 1) % 2, t - WB_LAG)

        @block.scalar
        def _(act):
            def hi_of_x(b, par):
                act.wait_ge(s_xt, b + 1)
                nc.scalar.activation(xT_hi[:, par], att[:, 1], ACT.Copy).then_inc(s_xhi, 1)

            def hi_of_kq(b):
                act.wait_ge(s_k, b + 1)
                nc.scalar.activation(kT_hi[:], att[:, 0], ACT.Identity, bias=bias[:, 1:2]).then_inc(s_khi, 1)
                act.wait_ge(s_q, b + 1)
                nc.scalar.activation(qT_hi[:], att[:, 1], ACT.Identity, bias=bqs[:]).then_inc(s_qhi, 1)

            def hi_of_v(b):
                act.wait_ge(s_v, b + 1)
                nc.scalar.activation(v_hi[:].rearrange("p (a k) d -> p a k d", a=2),
                                     att[:, :, 0:2 * VG].rearrange("p a (k c) -> p a k c", k=2)[:, :, :, 0:D],
                                     ACT.Copy).then_inc(s_vhi, 1)

            def weights_kept(b):
                act.wait_ge(s_wt, b + 1)
                nc.scalar.activation(wT[:], wrow[0:2 * R, :], ACT.Copy).then_inc(s_wts, 1)

            def hidden_hi(b, par, t):
                M = ROWS[t % NT]
                act.wait_ge(s_c, tile(b, t) + 1)
                if not (isinstance(b, int) and b == 0 and t < RING):
                    act.wait_ge(s_d, tile(b, t) - RING + 1)
                nc.scalar.activation(h_hi[0:M, ring(par, t, RING)], hid[0:M, ring(par, t, 2)], ACT.Copy).then_inc(s_hhi, 1)

            def acc_kept(b):
                act.wait_ge(s_d, tile(b, NT))
                nc.scalar.activation(accT[:], acc[:], ACT.Identity, bias=bias[:, 2:3]).then_inc(s_accs, 1)

            act.wait_ge(s_wqs, 2)
            nc.scalar.activation(wq_hi[:, 0:D], wqs[:], ACT.Copy)
            nc.scalar.activation(wq_hi[:, D:2 * D + VG], wq_raw[:, D:2 * D + VG], ACT.Copy).then_inc(s_wqhi, 1)
            act.wait_ge(s_up[0], 16)
            nc.scalar.activation(wup_hi[:, 0], wup_raw[:, 0], ACT.Copy).then_inc(s_uphi, 1)
            hi_of_x(0, 0)
            hi_of_kq(0)
            hi_of_v(0)
            for c in range(1, CH):
                act.wait_ge(s_up[c], 16)
                nc.scalar.activation(wup_hi[:, c], wup_raw[:, c], ACT.Copy).then_inc(s_uphi, 1)
            act.wait_ge(s_dn, 16)
            for c in range(2):
                w = NT * D // 2
                nc.scalar.activation(wdn_hi[:, c * w:(c + 1) * w], wdn_raw[:, c * w:(c + 1) * w],
                                     ACT.Copy).then_inc(s_dnhi, 1)
            act.wait_ge(s_sel, 16)
            nc.scalar.activation(sel[:], sel_raw[:], ACT.Copy).then_inc(s_selr, 1)

            def body(b, par, pair, first, last):
                act.wait_ge(s_gate, b * GATE_STEPS + 6)
                nc.scalar.activation(eout[:], ein[:], ACT.Exp).then_inc(s_gexp, 1)
                for j in range(TJ):
                    act.wait_ge(s_max, b * TJ + j + 1)
                    nc.scalar.activation(probs[:, j], att[:, j % 2], ACT.Exp, bias=nmax[:, j:j + 1],
                                         accum_out=psums[:, j:j + 1]).then_inc(s_exp, 1)
                for t in range(NT):
                    M = ROWS[t]
                    act.wait_ge(s_g, tile(b, t) + 1)
                    nc.scalar.activation(silu[0:M, ring(par, t, 2)], gu[0:M, 2 * ring(par, t, 2)],
                                         ACT.Silu).then_inc(s_silu, 1)
                    if t == WB_LAG:
                        weights_kept(b)
                    if not first or t >= WB_LAG:
                        hidden_hi(b, par, t - WB_LAG)
                    if 3 <= t <= 6:
                        act.wait_ge(s_pt, b * TJ + t - 2)
                        nc.scalar.activation(pT_hi[:, :, (t - 3) * P:(t - 2) * P],
                                             att[:, (t - 3) % 2].rearrange("p (s q) -> p s q", s=TJ),
                                             ACT.Copy).then_inc(s_pthi, 1)
                    if t == 4 and not first:
                        acc_kept(b - 1)
                    if not last:
                        if t == 10:
                            hi_of_x(b + 1, 1 - par)
                        if t == 11:
                            hi_of_kq(b + 1)
                        if t == 12:
                            hi_of_v(b + 1)

            bodies(act, body)
            for t in range(NT, NT + WB_LAG):
                hidden_hi(B - 1, (B - 1) % 2, t - WB_LAG)
            acc_kept(B - 1)

        @block.vector
        def _(dve):
            def statistics(par, nth):
                dve.wait_ge(s_x[par], (nth + 1) * 16)
                for j in range(TJ):
                    ins = nc.vector.bn_stats(stats[:, j], xs[:, par, j * D:(j + 1) * D])
                ins.then_inc(s_st, 1)

            def moments(b):
                for j in range(TJ):
                    ins = nc.vector.bn_aggr(mv[:, j], stats[:, j])
                ins.then_inc(s_mv, 1)
                dve.wait_ge(s_mv, b + 1)
                nc.vector.tensor_scalar(veps[:], mv[:, :, 1], EPS, None, ALU.add).then_inc(s_ve, 1)

            def normalise(b, par):
                dve.wait_ge(s_rstd, b + 1)
                for j in range(TJ):
                    ins = nc.vector.tensor_scalar(xn[:, j * D:(j + 1) * D], xs[:, par, j * D:(j + 1) * D],
                                                  mv[:, j, 0:1], rstd[:, j:j + 1], ALU.subtract, ALU.mult)
                ins.then_inc(s_xn, 1)

            def lo_of_x(b, par):
                dve.wait_ge(s_xhi, b + 1)
                nc.vector.tensor_tensor(xT_lo[:, par], att[:, 1], xT_hi[:, par].bitcast(F32),
                                        ALU.subtract).then_inc(s_xlo, 1)

            def lo_of_kq(b):
                dve.wait_ge(s_khi, b + 1)
                nc.vector.scalar_tensor_tensor(out=kT_lo[:], in0=att[:, 0], scalar=bias[:, 1:2], in1=kT_hi[:].bitcast(F32),
                                               op0=ALU.add, op1=ALU.subtract).then_inc(s_klo, 1)
                dve.wait_ge(s_qhi, b + 1)
                nc.vector.scalar_tensor_tensor(out=qT_lo[:], in0=att[:, 1], scalar=bqs[:], in1=qT_hi[:].bitcast(F32),
                                               op0=ALU.add, op1=ALU.subtract).then_inc(s_qlo, 1)

            def lo_of_v_and_logits(b):
                va = att[:, :, 0:2 * VG].rearrange("p a (k c) -> p a k c", k=2)
                dve.wait_ge(s_vhi, b + 1)
                nc.vector.tensor_copy(logit[:].rearrange("p (a k) r -> p a k r", a=2),
                                      va[:, :, :, D:D + R]).then_inc(s_gate, 1)
                nc.vector.tensor_tensor(v_lo[:].rearrange("p (a k) d -> p a k d", a=2), va[:, :, :, 0:D],
                                        v_hi[:].bitcast(F32).rearrange("p (a k) d -> p a k d", a=2),
                                        ALU.subtract).then_inc(s_vlo, 1)

            def router_before_exp(b):
                def step(k):
                    dve.wait_ge(s_gate, b * GATE_STEPS + k)

                step(1)
                le = logit[:, :, 0:E]
                nc.vector.tensor_reduce(lmax[:], le, AX.X, ALU.max).then_inc(s_gate, 1)
                nc.vector.tensor_tensor(diff[:], le.unsqueeze(2).broadcast_to([P, TJ, E, E]),
                                        le.unsqueeze(3).broadcast_to([P, TJ, E, E]), ALU.subtract).then_inc(s_gate, 1)
                step(2)
                nc.vector.tensor_tensor(ein[:, :, 0:E], le, lmax[:].unsqueeze(2).broadcast_to([P, TJ, E]),
                                        ALU.subtract).then_inc(s_gate, 1)
                step(3)
                nc.vector.tensor_tensor(beats[:], diff[:],
                                        tie.rearrange("p (a c) -> p a c", a=E).unsqueeze(1).broadcast_to([P, TJ, E, E]),
                                        ALU.is_gt).then_inc(s_gate, 1)
                nc.vector.tensor_scalar(ein[:, :, E:R], logit[:, :, E:R], -1.0, 87.0, ALU.mult, ALU.min).then_inc(s_gate, 1)

            def router_after_exp(b):
                def step(k):
                    dve.wait_ge(s_gate, b * GATE_STEPS + k)

                step(5)
                nc.vector.tensor_reduce(rank[:], beats[:], AX.X, ALU.add).then_inc(s_gate, 1)
                dve.wait_ge(s_gexp, b + 1)
                nc.vector.tensor_reduce(den[:, :, 0:1], eout[:, :, 0:E], AX.X, ALU.add)
                nc.vector.tensor_scalar(den[:, :, 1:2], eout[:, :, E:R], 1.0, None, ALU.add).then_inc(s_gate, 1)
                step(7)
                nc.vector.scalar_tensor_tensor(out=wtop[:], in0=rank[:], scalar=float(K_TOP), in1=eout[:, :, 0:E],
                                               op0=ALU.is_lt, op1=ALU.mult).then_inc(s_gate, 1)
                step(8)
                nc.vector.reciprocal(rden[:], den[:]).then_inc(s_gate, 1)
                step(10)
                nc.vector.tensor_tensor(wts[:, :, 0:E], wtop[:], rden[:, :, 0:1].broadcast_to([P, TJ, E]), ALU.mult)
                nc.vector.tensor_copy(wts[:, :, E:R], rden[:, :, 1:2]).then_inc(s_gate, 1)
                step(11)
                nc.vector.tensor_copy(wsplit[:, :, 0:R], wts[:]).then_inc(s_split, 1)
                dve.wait_ge(s_split, b + 1)
                nc.vector.tensor_tensor(wsplit[:, :, R:2 * R], wts[:], wsplit[:, :, 0:R].bitcast(F32),
                                        ALU.subtract).then_inc(s_gate, 1)

            def row_max(b, j):
                dve.wait_ge(s_sc, b * TJ + j + 1)
                nc.vector.tensor_reduce(nmax[:, j:j + 1], att[:, j % 2], AX.X, ALU.max, negate=True).then_inc(s_max, 1)

            def scale_probs(b, j):
                dve.wait_ge(s_exp, b * TJ + j + 1)
                nc.vector.reciprocal(pinv[:, j:j + 1], psums[:, j:j + 1]).then_inc(s_pinv, 1)
                dve.wait_ge(s_pinv, b * TJ + j + 1)
                nc.vector.tensor_scalar(probs[:, j], probs[:, j], pinv[:, j:j + 1], None, ALU.mult).then_inc(s_pn, 1)

            def lo_of_probs(b, j):
                dve.wait_ge(s_pthi, b * TJ + j + 1)
                nc.vector.tensor_tensor(pT_lo[:, :, j * P:(j + 1) * P],
                                        att[:, j % 2].rearrange("p (s q) -> p s q", s=TJ),
                                        pT_hi[:, :, j * P:(j + 1) * P].bitcast(F32), ALU.subtract).then_inc(s_ptlo, 1)

            def product(b, par, t):
                M = ROWS[t]
                dve.wait_ge(s_silu, tile(b, t) + 1)
                dve.wait_ge(s_u, tile(b, t) + 1)
                nc.vector.tensor_tensor(prod[0:M, ring(par, t, RING)], silu[0:M, ring(par, t, 2)],
                                        gu[0:M, 2 * ring(par, t, 2) + 1], ALU.mult).then_inc(s_b, 1)

            def weighted(b, par, t):
                M = ROWS[t % NT]
                n = tile(b, t)
                dve.wait_ge(s_wb, n + 1)
                dve.wait_ge(s_b, n + 1)
                if not (isinstance(b, int) and b == 0 and t < 2):
                    dve.wait_ge(s_hlo, n - 1)
                nc.vector.tensor_tensor(hid[0:M, ring(par, t, 2)], prod[0:M, ring(par, t, RING)], wrow[0:M, :],
                                        ALU.mult).then_inc(s_c, 1)

            def result(b, par):
                dve.wait_ge(s_ot, b + 1)
                dve.wait_ge(s_store, (b + 1) * 16)
                nc.vector.tensor_tensor(res[:], att[:, 0], xs[:, par], ALU.add).then_inc(s_out, 1)

            statistics(0, 0)
            dve.wait_ge(s_st, 1)
            moments(0)
            dve.wait_ge(s_wq, 32)
            nc.vector.tensor_scalar(wqs[:], wq_raw[:, 0:D], SCALE, None, ALU.mult).then_inc(s_wqs, 1)
            nc.vector.tensor_scalar(bqs[:], bias[:, 0:1], SCALE, None, ALU.mult).then_inc(s_wqs, 1)
            normalise(0, 0)
            dve.wait_ge(s_wqhi, 1)
            dve.wait_ge(s_wqs, 1)
            nc.vector.tensor_tensor(wq_lo[:, 0:D], wqs[:], wq_hi[:, 0:D].bitcast(F32), ALU.subtract)
            nc.vector.tensor_tensor(wq_lo[:, D:2 * D + VG], wq_raw[:, D:2 * D + VG],
                                    wq_hi[:, D:2 * D + VG].bitcast(F32), ALU.subtract).then_inc(s_wqlo, 1)
            lo_of_x(0, 0)
            lo_of_kq(0)
            dve.wait_ge(s_cst, 16)
            lo_of_v_and_logits(0)
            router_before_exp(0)

            def up_lo(c):
                dve.wait_ge(s_uphi, c + 1)
                nc.vector.tensor_tensor(wup_lo[:, c, CW:2 * CW], wup_raw[:, c, CW:2 * CW],
                                        wup_hi[:, c, CW:2 * CW].bitcast(F32), ALU.subtract).then_inc(s_uplo_v, 1)

            up_lo(0)

            def body(b, par, pair, first, last):
                row_max(b, 0)
                row_max(b, 1)
                row_max(b, 2)
                row_max(b, 3)
                if first:
                    for c in range(1, CH):
                        up_lo(c)
                router_after_exp(b)
                for t in range(NT):
                    if t < 4:
                        scale_probs(b, t)
                    if t == 9 and not last:
                        dve.wait_ge(s_st, b + 2)
                    product(b, par, t)
                    if t == 9 and not last:
                        moments(b + 1)
                    if not first or t >= WB_LAG:
                        weighted(b, par, t - WB_LAG)
                    if 3 <= t <= 6:
                        lo_of_probs(b, t - 3)
                    if t == 6 and not first:
                        result(b - 1, 1 - par)
                    if not last:
                        if t == 8:
                            statistics(1 - par, pair)
                        if t == 9:
                            normalise(b + 1, 1 - par)
                        if t == 10:
                            lo_of_x(b + 1, 1 - par)
                        if t == 11:
                            lo_of_kq(b + 1)
                        if t == 12:
                            lo_of_v_and_logits(b + 1)
                        if t == 13:
                            router_before_exp(b + 1)

            bodies(dve, body)
            for t in range(NT, NT + WB_LAG):
                weighted(B - 1, (B - 1) % 2, t - WB_LAG)
            result(B - 1, (B - 1) % 2)

        @block.tensor
        def _(pe):
            def three(out_ap, w_hi, w_lo, m_hi, m_lo, start=True, stop=True):
                nc.tensor.matmul(out_ap, w_hi, m_hi, start=start, stop=False, skip_group_check=True)
                nc.tensor.matmul(out_ap, w_hi, m_lo, start=False, stop=False, skip_group_check=True)
                return nc.tensor.matmul(out_ap, w_lo, m_hi, start=False, stop=stop, skip_group_check=True)

            def turn_x(b):
                pe.wait_ge(s_xn, b + 1)
                if isinstance(b, int) and b == 0:
                    pe.wait_ge(s_cst, 16)
                for j in range(TJ):
                    ins = nc.tensor.transpose(att[:, 1, j * P:(j + 1) * P], xn[:, j * D:(j + 1) * D], ident)
                ins.then_inc(s_xt, 1)

            def keys_queries(b, par):
                pe.wait_ge(s_xlo, b + 1)
                m = xT_hi[:, par], xT_lo[:, par]
                three(att[:, 0], wq_hi[:, D:2 * D], wq_lo[:, D:2 * D], *m).then_inc(s_k, 1)
                three(att[:, 1], wq_hi[:, 0:D], wq_lo[:, 0:D], *m).then_inc(s_q, 1)

            def values_logits(b, par):
                pe.wait_ge(s_klo, b + 1)
                pe.wait_ge(s_qlo, b + 1)
                wv = slice(2 * D, 2 * D + VG)
                for j in range(TJ):
                    o = att[:, j // 2, (j % 2) * VG:(j % 2 + 1) * VG]
                    cols = slice(j * P, (j + 1) * P)
                    ins = three(o, xT_hi[:, par, cols], xT_lo[:, par, cols], wq_hi[:, wv], wq_lo[:, wv])
                ins.then_inc(s_v, 1)

            def scores(b, j):
                if j == 0:
                    pe.wait_ge(s_vlo, b + 1)
                if j >= 2:
                    pe.wait_ge(s_exp, b * TJ + j - 1)
                q = slice(j * P, (j + 1) * P)
                three(att[:, j % 2], qT_hi[:, q], qT_lo[:, q], kT_hi[:], kT_lo[:]).then_inc(s_sc, 1)

            def turn_probs(b, j):
                pe.wait_ge(s_pn, b * TJ + j + 1)
                if j < 2:
                    pe.wait_ge(s_exp, b * TJ + j + 3)
                else:
                    pe.wait_ge(s_ptlo, b * TJ + j - 1)
                for s in range(TJ):
                    ins = nc.tensor.transpose(att[:, j % 2, s * P:(s + 1) * P], probs[:, j, s * P:(s + 1) * P], ident)
                ins.then_inc(s_pt, 1)

            def attend(b):
                pe.wait_ge(s_ptlo, (b + 1) * TJ)
                for s in range(TJ):
                    ins = three(acc[:], v_hi[:, s], v_lo[:, s], pT_hi[:, s], pT_lo[:, s], start=False, stop=False)
                ins.then_inc(s_av, 1)

            def turn_weights(b, first):
                pe.wait_ge(s_gate, (b + 1) * GATE_STEPS)
                if not first:
                    pe.wait_ge(s_c, tile(b, 0))
                for j in range(TJ):
                    ins = nc.tensor.transpose(wrow[0:2 * R, j * P:(j + 1) * P], wsplit[:, j].bitcast(F32), ident)
                ins.then_inc(s_wt, 1)

            def turn_result(b, first=False):
                pe.wait_ge(s_accs, b + 1)
                for j in range(TJ):
                    ins = nc.tensor.transpose(att[:, 0, j * P:(j + 1) * P], accT[:, j * P:(j + 1) * P], ident)
                ins.then_inc(s_ot, 1)

            def gate_up(b, par, t, first):
                M, n, g = ROWS[t], tile(b, t), 2 * ring(par, t, 2)
                c, cols = divmod(t * P, CW)
                m = xT_hi[:, par], xT_lo[:, par]
                if first:
                    need = -(-min((t + 1) * P, HID) // CW)
                    pe.wait_ge(s_uplo, need)
                    pe.wait_ge(s_uplo_v, need)
                if not (first and t < 2):
                    pe.wait_ge(s_b, n - 1)
                for which, ready in ((0, s_g), (1, s_u)):
                    o = gu[0:M, g + which]
                    whi, wlo = up_columns(t, which)
                    three(o, whi, wlo, *m).then_inc(ready, 1)

            def up_columns(t, which):
                c0 = (2 * t + which) * P - (which * (P - ROWS[t]))
                return (wup_hi[:].rearrange("p c n -> p (c n)")[:, c0:c0 + ROWS[t]],
                        wup_lo[:].rearrange("p c n -> p (c n)")[:, c0:c0 + ROWS[t]])

            def weight_rows(b, par, t):
                M = ROWS[t % NT]
                tt = t % NT
                n = tile(b, t)
                if tt == 0:
                    pe.wait_ge(s_wts, b + 1 if t >= 0 else b)
                if not (isinstance(b, int) and b == 0 and t == 0):
                    pe.wait_ge(s_c, n)
                nc.tensor.matmul(wrow[0:M, :], sel[:, tt * P:tt * P + M], wT[:], start=True, stop=True).then_inc(s_wb, 1)

            def down(b, par, t):
                M, tt = ROWS[t % NT], t % NT
                slot = ring(par, t, RING)
                if tt == 0 and not (isinstance(b, int) and b == 0):
                    pe.wait_ge(s_accs, b)
                pe.wait_ge(s_hlo, tile(b, t) + 1)
                cols = slice(tt * D, (tt + 1) * D)
                three(acc[:], wdn_hi[0:M, cols], wdn_lo[0:M, cols], h_hi[0:M, slot], h_lo[0:M, slot],
                      start=(tt == 0), stop=(tt == NT - 1)).then_inc(s_d, 1)

            turn_x(0)
            pe.wait_ge(s_wqlo, 1)
            keys_queries(0, 0)
            values_logits(0, 0)

            def body(b, par, pair, first, last):
                scores(b, 0)
                scores(b, 1)
                for t in range(NT):
                    if t == WB_LAG:
                        turn_weights(b, first)
                    gate_up(b, par, t, first)
                    if t == 0:
                        scores(b, 2)
                        scores(b, 3)
                    if first and t == WB_LAG:
                        pe.wait_ge(s_selr, 1)
                    if first and t == DOWN_LAG:
                        pe.wait_ge(s_dnlo, 2)
                    if not first or t >= WB_LAG:
                        weight_rows(b, par, t - WB_LAG)
                    if 2 <= t <= 5:
                        turn_probs(b, t - 2)
                    if not first or t >= DOWN_LAG:
                        down(b, par, t - DOWN_LAG)
                    if t == 6 and not first:
                        pe.wait_ge(s_ptlo, b * TJ + 3)
                        turn_result(b - 1)
                    if t == 7:
                        attend(b)
                    if not last:
                        if t == 10:
                            turn_x(b + 1)
                        if t == 11:
                            if not first:
                                pe.wait_ge(s_out, b)
                            keys_queries(b + 1, 1 - par)
                        if t == 12:
                            values_logits(b + 1, 1 - par)

            bodies(pe, body)
            b, par = B - 1, (B - 1) % 2
            for t in range(NT, NT + DOWN_LAG):
                if t < NT + WB_LAG:
                    weight_rows(b, par, t - WB_LAG)
                down(b, par, t - DOWN_LAG)
            turn_result(b)


_INS = ["x", "w_qkvr", "biases", "w_up", "w_down", "consts", "select"]


def kernel(**inputs):
    import numpy as _np
    import concourse.bacc as _bacc
    from concourse import mybir as _mybir
    from concourse.bass_utils import run_bass_kernel_spmd as _run

    a = {k.replace("L0_attn_", "").replace("L0_ffn_", "f_"): _np.asarray(v) for k, v in inputs.items()}
    f32 = _np.float32
    pad = _np.zeros((D, 1), f32)
    w_qkvr = _np.concatenate([a["Wq"], a["Wk"], a["Wv"], a["f_gate_w"].T, a["f_shared_expert_gate_w"].T, pad], axis=1)
    biases = _np.stack([a["bq"], a["bk"], a["bv"]], axis=1)
    gu = a["f_experts_gate_up"]
    gate = _np.concatenate([gu[:, :I].reshape(E * I, D), a["f_shared_gate_w"]]).T
    up = _np.concatenate([gu[:, I:].reshape(E * I, D), a["f_shared_up_w"]]).T
    w_up = _np.concatenate([m[:, t * P:t * P + ROWS[t]] for t in range(NT) for m in (gate, up)], axis=1)
    w_up = w_up.reshape(P, CH, 2 * CW)
    down = _np.concatenate([a["f_experts_down"].transpose(0, 2, 1).reshape(E * I, D), a["f_shared_down_w"].T,
                            _np.zeros((NT * P - HID, D), f32)])
    w_down = down.reshape(NT, P, D).transpose(1, 0, 2).reshape(P, NT * D)
    tie = _np.zeros((E, E), f32)
    for e in range(E):
        tie[e, :e] = -1.2e-38
    consts = _np.concatenate([_np.eye(P, dtype=f32), _np.tile(tie.reshape(1, E * E), (P, 1))], axis=1)
    select = _np.zeros((2 * R, NT * P), f32)
    for row in range(HID):
        e = min(row // I, E)
        select[e, row] = select[R + e, row] = 1.0

    arrays = dict(zip(_INS, [a["x"], w_qkvr, biases, w_up, w_down, consts, select]))
    nc = _bacc.Bacc("TRN2", target_bir_lowering=False, num_devices=1)
    feed, args = {}, []
    for name in _INS:
        m = _np.ascontiguousarray(arrays[name])
        feed[f"in_{name}_dram"] = m
        args.append(nc.dram_tensor(f"in_{name}_dram", m.shape, _mybir.dt.from_np(m.dtype), kind="ExternalInput").ap())
    out = nc.dram_tensor("out_dram", (B, S, D), F32, kind="ExternalOutput").ap()
    moe_attention_layer(nc, *args, out)
    return _run(nc, [feed], core_ids=[0]).results[0]["out_dram"]
```

```python
from contextlib import ExitStack

import concourse.bass as bass
from concourse import mybir

F32 = mybir.dt.float32
F32R = mybir.dt.float32r
ALU = mybir.AluOpType
ACT = mybir.ActivationFunctionType
AX = mybir.AxisListType

P = 128
B, S, D = 8, 512, 128
TJ = S // P
E, I, SI = 8, 176, 352
K_TOP = 2
R = E + 1
HID = E * I + SI
PE_ROWS = P // E
ET = I // PE_ROWS
NT = -(-HID // P)
ROWS = [min(P, HID - P * t) for t in range(NT)]
CH = 4
CW = HID // CH
VG = D + R + 1
SCALE = 1.0 / float(D) ** 0.5
EPS = 1e-5
WB_LAG, HID_LAG, DOWN_LAG = 3, 4, 6
RING = 7
HID_RING = 4
GATE_STEPS = 12


def moe_attention_layer(nc, x, w_qkvr, biases, w_up, w_down, consts, select, out):
    x_v = x.rearrange("b (p j) d -> b p (j d)", j=TJ)
    out_v = out.rearrange("b (p j) d -> b p (j d)", j=TJ)

    with ExitStack() as ctx:
        def sb(name, shape, dt=F32):
            return ctx.enter_context(nc.sbuf_tensor(name, shape, dt))

        def pb(name, shape):
            return ctx.enter_context(nc.psum_tensor(name, shape, F32))

        def sem(name):
            return ctx.enter_context(nc.semaphore(name))

        wq_raw = sb("wq_raw", [P, 2 * D + VG])
        wqs = sb("wqs", [P, D])
        bias = sb("bias", [P, 3])
        bqs = sb("bqs", [P, 1])
        wup_raw = sb("wup_raw", [P, CH, 2 * CW])
        wdn_raw = sb("wdn_raw", [P, NT * D])
        cst = sb("cst", [P, P + E * E])
        sel_raw = sb("sel_raw", [2 * R, 2 * P])
        wq_hi, wq_lo = sb("wq_hi", [P, 2 * D + VG], F32R), sb("wq_lo", [P, 2 * D + VG], F32R)
        wup_hi, wup_lo = sb("wup_hi", [P, CH, 2 * CW], F32R), sb("wup_lo", [P, CH, 2 * CW], F32R)
        wdn_hi, wdn_lo = sb("wdn_hi", [P, NT * D], F32R), sb("wdn_lo", [P, NT * D], F32R)
        sel = sb("sel", [2 * R, 2 * P], F32R)
        ident = cst[:, 0:P]
        tie = cst[:, P:P + E * E]
        mhalf = sb("mhalf", [P, TJ])

        xs = sb("xs", [P, 2, S])
        xr = sb("xr", [P, 2, S])
        stats = sb("stats", [P, TJ, 6])
        mv = sb("mv", [P, TJ, 2])
        veps = sb("veps", [P, TJ])
        rstd = sb("rstd", [P, TJ])
        xn = sb("xn", [P, S])
        xT_hi, xT_lo = sb("xT_hi", [P, 2, S], F32R), sb("xT_lo", [P, 2, S], F32R)
        kT_hi, kT_lo = sb("kT_hi", [P, S], F32R), sb("kT_lo", [P, S], F32R)
        qT_hi, qT_lo = sb("qT_hi", [P, S], F32R), sb("qT_lo", [P, S], F32R)
        v_hi, v_lo = sb("v_hi", [P, TJ, D], F32R), sb("v_lo", [P, TJ, D], F32R)
        probs = sb("probs", [P, TJ, S])
        nmax = sb("nmax", [P, TJ])
        psums = sb("psums", [P, TJ])
        pinv = sb("pinv", [P, TJ])
        pT_hi, pT_lo = sb("pT_hi", [P, TJ, S], F32R), sb("pT_lo", [P, TJ, S], F32R)
        logit = sb("logit", [P, TJ, R])
        diff = sb("diff", [P, TJ, E, E])
        beats = sb("beats", [P, TJ, E, E])
        rank = sb("rank", [P, TJ, E])
        lmax = sb("lmax", [P, TJ])
        ein = sb("ein", [P, TJ, R])
        eout = sb("eout", [P, TJ, R])
        den = sb("den", [P, TJ, 2])
        rden = sb("rden", [P, TJ, 2])
        wtop = sb("wtop", [P, TJ, E])
        wts = sb("wts", [P, TJ, R])
        wsplit = sb("wsplit", [P, TJ, 2 * R], F32R)
        wT = sb("wT", [2 * R, 2, S], F32R)
        wshared = sb("wshared", [P, S])
        silu = sb("silu", [P, 2, S])
        prod = sb("prod", [P, RING, S])
        hid = sb("hid", [P, HID_RING, S])
        h_hi, h_lo = sb("h_hi", [P, RING, S], F32R), sb("h_lo", [P, RING, S], F32R)
        accT = sb("accT", [P, S])
        res = sb("res", [P, S])

        att = pb("att", [P, 2, S])
        gu = pb("gu", [P, 4, S])
        wrow = pb("wrow", [P, S])
        acc = pb("acc", [P, S])

        s_wq, s_cst, s_dn, s_sel, s_store = map(
            sem, ["qkv_loaded", "consts_loaded", "down_loaded", "select_loaded", "stored"])
        s_x = [sem("x_even_loaded"), sem("x_odd_loaded")]
        s_r = [sem("residual_even_loaded"), sem("residual_odd_loaded")]
        s_up = [sem(f"up_loaded{c}") for c in range(CH)]
        s_wqs, s_mhalf = sem("q_scaled"), sem("mhalf_set")
        s_wqhi, s_wqlo = sem("qkv_hi"), sem("qkv_lo")
        s_uphi, s_uplo, s_uplo_v = sem("up_hi"), sem("gate_lo"), sem("up_lo")
        s_dnhi, s_dnlo, s_selr = sem("down_hi"), sem("down_lo"), sem("select_rounded")
        s_xt, s_k, s_q, s_v, s_sc, s_pt, s_av, s_wt, s_ot = map(
            sem, ["xT_made", "k_made", "q_made", "v_made", "scores_made", "pT_made", "av_made",
                  "wT_made", "outT_turned"])
        s_g, s_u, s_wb, s_ws, s_d = map(sem, ["gate_made", "up_made", "wrow_made", "shared_row_made", "down_made"])
        s_gexp, s_exp, s_silu, s_xhi, s_khi, s_qhi, s_vhi, s_wts, s_pthi, s_accs, s_hhi = map(
            sem, ["router_exp", "probs_exp", "silu_made", "xT_hi_made", "k_hi_made", "q_hi_made",
                  "v_hi_made", "wT_kept", "pT_hi_made", "acc_kept", "h_hi_made"])
        s_wsh = sem("shared_weight_kept")
        s_st, s_mv, s_ve, s_xn, s_xlo, s_klo, s_qlo, s_vlo, s_gate, s_max, s_pinv, s_pn, s_ptlo, \
            s_b, s_c, s_out = map(
                sem, ["stats_made", "moments_made", "var_eps", "xn_made", "xT_lo_made", "k_lo_made",
                      "q_lo_made", "v_lo_made", "router_step", "max_made", "sum_inverted",
                      "probs_scaled", "pT_lo_made", "prod_made", "hid_made", "result_made"])
        s_split = sem("weights_hi")
        s_rstd, s_hlo = sem("rstd_made"), sem("h_lo_made")

        def tile(b, t):
            return b * NT + t

        def ring(par, t, size):
            return (NT * par + t) % size

        def bodies(eng, body):
            body(0, 0, 0, True, False)
            with eng.Fori(0, (B - 2) // 2) as i:
                body(i * 2 + 1, 1, i + 1, False, False)
                body(i * 2 + 2, 0, i + 1, False, False)
            body(B - 1, (B - 1) % 2, B // 2, False, True)

        block = ctx.enter_context(nc.Block())

        @block.sync
        def _(sp):
            sp.dma_start(xs[:, 0, :], x_v[0]).then_inc(s_x[0], 16)
            sp.dma_start(cst[:], consts).then_inc(s_cst, 16)
            sp.dma_start(wq_raw[:], w_qkvr).then_inc(s_wq, 16)
            sp.dma_start(bias[:], biases).then_inc(s_wq, 16)
            sp.dma_start(wup_raw[:, 0], w_up[:, 0]).then_inc(s_up[0], 16)
            sp.dma_start(sel_raw[:], select).then_inc(s_sel, 16)
            for c in range(1, CH):
                sp.dma_start(wup_raw[:, c], w_up[:, c]).then_inc(s_up[c], 16)
            sp.dma_start(wdn_raw[:], w_down).then_inc(s_dn, 16)
            sp.dma_start(xs[:, 1, :], x_v[1]).then_inc(s_x[1], 16)
            for b in range(2):
                sp.dma_start(xr[:, b, :], x_v[b]).then_inc(s_r[b], 16)
            sp.sem_inc(s_store, 16)

            def batch_of(v, b):
                return v[b] if isinstance(b, int) else v[bass.ds(b, 1)].rearrange("a p n -> (a p) n")

            def load_and_store(b, par, more):
                if more:
                    sp.wait_ge(s_xn, b + 1)
                    sp.dma_start(xs[:, par, :], batch_of(x_v, b + 2)).then_inc(s_x[par], 16)
                sp.wait_ge(s_out, b + 1)
                sp.dma_start(batch_of(out_v, b), res[:]).then_inc(s_store, 16)
                if more:
                    sp.dma_start(xr[:, par, :], batch_of(x_v, b + 2)).then_inc(s_r[par], 16)

            with sp.Fori(0, (B - 2) // 2) as i:
                load_and_store(i * 2, 0, True)
                load_and_store(i * 2 + 1, 1, True)
            load_and_store(B - 2, 0, False)
            load_and_store(B - 1, 1, False)
            sp.wait_ge(s_store, 16 * (B + 1))

        @block.gpsimd
        def _(pool):
            nc.gpsimd.memset(mhalf[:], -0.5).then_inc(s_mhalf, 1)

            def norm(b):
                pool.wait_ge(s_ve, b + 1)
                if isinstance(b, int) and b == 0:
                    pool.wait_ge(s_mhalf, 1)
                nc.gpsimd.tensor_tensor(rstd[:], veps[:], mhalf[:], ALU.pow).then_inc(s_rstd, 1)

            norm(0)
            for c in range(CH):
                pool.wait_ge(s_uphi, c + 1)
                nc.gpsimd.tensor_tensor(wup_lo[:, c, 0:CW], wup_raw[:, c, 0:CW],
                                        wup_hi[:, c, 0:CW].bitcast(F32), ALU.subtract).then_inc(s_uplo, 1)
            for c in range(2):
                w = NT * D // 2
                pool.wait_ge(s_dnhi, c + 1)
                nc.gpsimd.tensor_tensor(wdn_lo[:, c * w:(c + 1) * w], wdn_raw[:, c * w:(c + 1) * w],
                                        wdn_hi[:, c * w:(c + 1) * w].bitcast(F32), ALU.subtract).then_inc(s_dnlo, 1)

            def hidden_lo(b, par, t):
                M = ROWS[t % NT]
                pool.wait_ge(s_hhi, tile(b, t) + 1)
                nc.gpsimd.tensor_tensor(h_lo[0:M, ring(par, t, RING)], hid[0:M, ring(par, t, HID_RING)],
                                        h_hi[0:M, ring(par, t, RING)].bitcast(F32), ALU.subtract).then_inc(s_hlo, 1)

            def scale_probs(b, j):
                pool.wait_ge(s_pinv, b * TJ + j + 1)
                nc.gpsimd.tensor_tensor(probs[:, j], probs[:, j], pinv[:, j:j + 1].broadcast_to([P, S]),
                                        ALU.mult).then_inc(s_pn, 1)

            def body(b, par, pair, first, last):
                for t in range(NT):
                    if t < TJ:
                        scale_probs(b, t)
                    if not first or t >= HID_LAG:
                        hidden_lo(b, par, t - HID_LAG)
                    if t == 6 and not last:
                        norm(b + 1)

            bodies(pool, body)
            for t in range(NT, NT + HID_LAG):
                hidden_lo(B - 1, (B - 1) % 2, t - HID_LAG)

        @block.scalar
        def _(act):
            def hi_of_x(b, par):
                act.wait_ge(s_xt, b + 1)
                nc.scalar.activation(xT_hi[:, par], att[:, 0], ACT.Copy).then_inc(s_xhi, 1)

            def hi_of_kq(b):
                act.wait_ge(s_k, b + 1)
                nc.scalar.activation(kT_hi[:], att[:, 1], ACT.Identity, bias=bias[:, 1:2]).then_inc(s_khi, 1)
                act.wait_ge(s_q, b + 1)
                nc.scalar.activation(qT_hi[:], att[:, 0], ACT.Identity, bias=bqs[:]).then_inc(s_qhi, 1)

            def hi_of_v(b):
                act.wait_ge(s_v, b + 1)
                nc.scalar.activation(v_hi[:].rearrange("p (a k) d -> p a k d", a=2),
                                     att[:, :, 0:2 * VG].rearrange("p a (k c) -> p a k c", k=2)[:, :, :, 0:D],
                                     ACT.Copy).then_inc(s_vhi, 1)

            def weights_kept(b, par):
                act.wait_ge(s_wt, b + 1)
                nc.scalar.activation(wT[:, par], att[0:2 * R, 0], ACT.Copy).then_inc(s_wts, 1)

            def shared_weight(b, first):
                act.wait_ge(s_ws, b + 1)
                if not first:
                    act.wait_ge(s_c, tile(b, 0))
                nc.scalar.activation(wshared[:], att[:, 0], ACT.Copy).then_inc(s_wsh, 1)

            def hidden_hi(b, par, t):
                M = ROWS[t % NT]
                act.wait_ge(s_c, tile(b, t) + 1)
                if not (isinstance(b, int) and b == 0 and t < RING):
                    act.wait_ge(s_d, tile(b, t) - RING + 1)
                nc.scalar.activation(h_hi[0:M, ring(par, t, RING)], hid[0:M, ring(par, t, HID_RING)], ACT.Copy).then_inc(s_hhi, 1)

            def acc_kept(b):
                act.wait_ge(s_d, tile(b, NT))
                nc.scalar.activation(accT[:], acc[:], ACT.Identity, bias=bias[:, 2:3]).then_inc(s_accs, 1)

            act.wait_ge(s_wqs, 2)
            nc.scalar.activation(wq_hi[:, 0:D], wqs[:], ACT.Copy)
            nc.scalar.activation(wq_hi[:, D:2 * D + VG], wq_raw[:, D:2 * D + VG], ACT.Copy).then_inc(s_wqhi, 1)
            act.wait_ge(s_up[0], 16)
            nc.scalar.activation(wup_hi[:, 0], wup_raw[:, 0], ACT.Copy).then_inc(s_uphi, 1)
            hi_of_x(0, 0)
            hi_of_kq(0)
            hi_of_v(0)
            for c in range(1, CH):
                act.wait_ge(s_up[c], 16)
                nc.scalar.activation(wup_hi[:, c], wup_raw[:, c], ACT.Copy).then_inc(s_uphi, 1)
            act.wait_ge(s_dn, 16)
            for c in range(2):
                w = NT * D // 2
                nc.scalar.activation(wdn_hi[:, c * w:(c + 1) * w], wdn_raw[:, c * w:(c + 1) * w],
                                     ACT.Copy).then_inc(s_dnhi, 1)
            act.wait_ge(s_sel, 16)
            nc.scalar.activation(sel[:], sel_raw[:], ACT.Copy).then_inc(s_selr, 1)

            def body(b, par, pair, first, last):
                for j in range(TJ):
                    if j == 2:
                        if not first:
                            hidden_hi(b, par, -1 - HID_LAG)
                        act.wait_ge(s_gate, b * GATE_STEPS + 6)
                        nc.scalar.activation(eout[:], ein[:], ACT.Exp).then_inc(s_gexp, 1)
                    act.wait_ge(s_max, b * TJ + j + 1)
                    nc.scalar.activation(probs[:, j], att[:, j % 2], ACT.Exp, bias=nmax[:, j:j + 1],
                                         accum_out=psums[:, j:j + 1]).then_inc(s_exp, 1)
                for t in range(NT):
                    M = ROWS[t]
                    act.wait_ge(s_g, tile(b, t) + 1)
                    nc.scalar.activation(silu[0:M, ring(par, t, 2)], gu[0:M, 2 * ring(par, t, 2)],
                                         ACT.Silu).then_inc(s_silu, 1)
                    if t != NT - 1 and (not first or t >= HID_LAG):
                        hidden_hi(b, par, t - HID_LAG)
                    if t == NT - 1 and last:
                        hidden_hi(b, par, t - HID_LAG)
                    if t == 2:
                        weights_kept(b, par)
                    if t == WB_LAG:
                        shared_weight(b, first)
                    if 3 <= t <= 6:
                        act.wait_ge(s_pt, b * TJ + t - 2)
                        nc.scalar.activation(pT_hi[:, :, (t - 3) * P:(t - 2) * P],
                                             att[:, (t - 2) % 2].rearrange("p (s q) -> p s q", s=TJ),
                                             ACT.Copy).then_inc(s_pthi, 1)
                    if t == DOWN_LAG - 1 and not first:
                        acc_kept(b - 1)
                    if not last:
                        if t == 8:
                            hi_of_x(b + 1, 1 - par)
                        if t == 9:
                            hi_of_kq(b + 1)
                        if t == 10:
                            hi_of_v(b + 1)

            bodies(act, body)
            for t in range(NT, NT + HID_LAG):
                hidden_hi(B - 1, (B - 1) % 2, t - HID_LAG)
            acc_kept(B - 1)

        @block.vector
        def _(dve):
            def statistics(par, nth):
                dve.wait_ge(s_x[par], (nth + 1) * 16)
                for j in range(TJ):
                    ins = nc.vector.bn_stats(stats[:, j], xs[:, par, j * D:(j + 1) * D])
                ins.then_inc(s_st, 1)

            def moments(b):
                for j in range(TJ):
                    ins = nc.vector.bn_aggr(mv[:, j], stats[:, j])
                ins.then_inc(s_mv, 1)
                dve.wait_ge(s_mv, b + 1)
                nc.vector.tensor_scalar(veps[:], mv[:, :, 1], EPS, None, ALU.add).then_inc(s_ve, 1)

            def normalise(b, par):
                dve.wait_ge(s_rstd, b + 1)
                for j in range(TJ):
                    ins = nc.vector.tensor_scalar(xn[:, j * D:(j + 1) * D], xs[:, par, j * D:(j + 1) * D],
                                                  mv[:, j, 0:1], rstd[:, j:j + 1], ALU.subtract, ALU.mult)
                ins.then_inc(s_xn, 1)

            def lo_of_x(b, par):
                dve.wait_ge(s_xhi, b + 1)
                nc.vector.tensor_tensor(xT_lo[:, par], att[:, 0], xT_hi[:, par].bitcast(F32),
                                        ALU.subtract).then_inc(s_xlo, 1)

            def lo_of_kq(b):
                dve.wait_ge(s_khi, b + 1)
                nc.vector.scalar_tensor_tensor(out=kT_lo[:], in0=att[:, 1], scalar=bias[:, 1:2], in1=kT_hi[:].bitcast(F32),
                                               op0=ALU.add, op1=ALU.subtract).then_inc(s_klo, 1)
                dve.wait_ge(s_qhi, b + 1)
                nc.vector.scalar_tensor_tensor(out=qT_lo[:], in0=att[:, 0], scalar=bqs[:], in1=qT_hi[:].bitcast(F32),
                                               op0=ALU.add, op1=ALU.subtract).then_inc(s_qlo, 1)

            def lo_of_v_and_logits(b):
                va = att[:, :, 0:2 * VG].rearrange("p a (k c) -> p a k c", k=2)
                dve.wait_ge(s_vhi, b + 1)
                nc.vector.tensor_copy(logit[:].rearrange("p (a k) r -> p a k r", a=2),
                                      va[:, :, :, D:D + R]).then_inc(s_gate, 1)
                nc.vector.tensor_tensor(v_lo[:].rearrange("p (a k) d -> p a k d", a=2), va[:, :, :, 0:D],
                                        v_hi[:].bitcast(F32).rearrange("p (a k) d -> p a k d", a=2),
                                        ALU.subtract).then_inc(s_vlo, 1)

            def router_before_exp(b):
                def step(k):
                    dve.wait_ge(s_gate, b * GATE_STEPS + k)

                step(1)
                le = logit[:, :, 0:E]
                nc.vector.tensor_reduce(lmax[:], le, AX.X, ALU.max).then_inc(s_gate, 1)
                nc.vector.tensor_tensor(diff[:], le.unsqueeze(2).broadcast_to([P, TJ, E, E]),
                                        le.unsqueeze(3).broadcast_to([P, TJ, E, E]), ALU.subtract).then_inc(s_gate, 1)
                step(2)
                nc.vector.tensor_tensor(ein[:, :, 0:E], le, lmax[:].unsqueeze(2).broadcast_to([P, TJ, E]),
                                        ALU.subtract).then_inc(s_gate, 1)
                step(3)
                nc.vector.tensor_tensor(beats[:], diff[:],
                                        tie.rearrange("p (a c) -> p a c", a=E).unsqueeze(1).broadcast_to([P, TJ, E, E]),
                                        ALU.is_gt).then_inc(s_gate, 1)
                nc.vector.tensor_scalar(ein[:, :, E:R], logit[:, :, E:R], -1.0, 87.0, ALU.mult, ALU.min).then_inc(s_gate, 1)

            def router_after_exp(b):
                def step(k):
                    dve.wait_ge(s_gate, b * GATE_STEPS + k)

                step(5)
                nc.vector.tensor_reduce(rank[:], beats[:], AX.X, ALU.add).then_inc(s_gate, 1)
                dve.wait_ge(s_gexp, b + 1)
                nc.vector.tensor_reduce(den[:, :, 0:1], eout[:, :, 0:E], AX.X, ALU.add)
                nc.vector.tensor_scalar(den[:, :, 1:2], eout[:, :, E:R], 1.0, None, ALU.add).then_inc(s_gate, 1)
                step(7)
                nc.vector.scalar_tensor_tensor(out=wtop[:], in0=rank[:], scalar=float(K_TOP), in1=eout[:, :, 0:E],
                                               op0=ALU.is_lt, op1=ALU.mult).then_inc(s_gate, 1)
                step(8)
                nc.vector.reciprocal(rden[:], den[:]).then_inc(s_gate, 1)
                step(10)
                nc.vector.tensor_tensor(wts[:, :, 0:E], wtop[:], rden[:, :, 0:1].broadcast_to([P, TJ, E]), ALU.mult)
                nc.vector.tensor_copy(wts[:, :, E:R], rden[:, :, 1:2]).then_inc(s_gate, 1)
                step(11)
                nc.vector.tensor_copy(wsplit[:, :, 0:R], wts[:]).then_inc(s_split, 1)
                dve.wait_ge(s_split, b + 1)
                nc.vector.tensor_tensor(wsplit[:, :, R:2 * R], wts[:], wsplit[:, :, 0:R].bitcast(F32),
                                        ALU.subtract).then_inc(s_gate, 1)

            def row_max(b, j):
                dve.wait_ge(s_sc, b * TJ + j + 1)
                nc.vector.tensor_reduce(nmax[:, j:j + 1], att[:, j % 2], AX.X, ALU.max, negate=True).then_inc(s_max, 1)

            def invert_sum(b, j):
                dve.wait_ge(s_exp, b * TJ + j + 1)
                nc.vector.reciprocal(pinv[:, j:j + 1], psums[:, j:j + 1]).then_inc(s_pinv, 1)

            def lo_of_probs(b, j):
                dve.wait_ge(s_pthi, b * TJ + j + 1)
                nc.vector.tensor_tensor(pT_lo[:, :, j * P:(j + 1) * P],
                                        att[:, (j + 1) % 2].rearrange("p (s q) -> p s q", s=TJ),
                                        pT_hi[:, :, j * P:(j + 1) * P].bitcast(F32), ALU.subtract).then_inc(s_ptlo, 1)

            def product(b, par, t):
                M = ROWS[t]
                dve.wait_ge(s_silu, tile(b, t) + 1)
                dve.wait_ge(s_u, tile(b, t) + 1)
                nc.vector.tensor_tensor(prod[0:M, ring(par, t, RING)], silu[0:M, ring(par, t, 2)],
                                        gu[0:M, 2 * ring(par, t, 2) + 1], ALU.mult).then_inc(s_b, 1)

            def weighted(b, par, t):
                M = ROWS[t % NT]
                n = tile(b, t)
                if t == 0:
                    dve.wait_ge(s_wb, b + 1)
                if t % NT == ET:
                    dve.wait_ge(s_wsh, b + 1 if t > 0 else b)
                dve.wait_ge(s_b, n + 1)
                if not (isinstance(b, int) and b == 0 and t < HID_RING):
                    dve.wait_ge(s_hlo, n - HID_RING + 1)
                nc.vector.tensor_tensor(hid[0:M, ring(par, t, HID_RING)], prod[0:M, ring(par, t, RING)],
                                        (wrow if t % NT < ET else wshared)[0:M, :],
                                        ALU.mult).then_inc(s_c, 1)

            def result(b, par, nth):
                dve.wait_ge(s_ot, b + 1)
                dve.wait_ge(s_r[par], (nth + 1) * 16)
                dve.wait_ge(s_store, (b + 1) * 16)
                nc.vector.tensor_tensor(res[:], att[:, 1], xr[:, par], ALU.add).then_inc(s_out, 1)

            statistics(0, 0)
            dve.wait_ge(s_st, 1)
            moments(0)
            dve.wait_ge(s_wq, 32)
            nc.vector.tensor_scalar(wqs[:], wq_raw[:, 0:D], SCALE, None, ALU.mult).then_inc(s_wqs, 1)
            nc.vector.tensor_scalar(bqs[:], bias[:, 0:1], SCALE, None, ALU.mult).then_inc(s_wqs, 1)
            normalise(0, 0)
            dve.wait_ge(s_wqhi, 1)
            dve.wait_ge(s_wqs, 1)
            nc.vector.tensor_tensor(wq_lo[:, 0:D], wqs[:], wq_hi[:, 0:D].bitcast(F32), ALU.subtract)
            nc.vector.tensor_tensor(wq_lo[:, D:2 * D + VG], wq_raw[:, D:2 * D + VG],
                                    wq_hi[:, D:2 * D + VG].bitcast(F32), ALU.subtract).then_inc(s_wqlo, 1)
            lo_of_x(0, 0)
            lo_of_kq(0)
            dve.wait_ge(s_cst, 16)
            lo_of_v_and_logits(0)
            router_before_exp(0)

            def up_lo(c):
                dve.wait_ge(s_uphi, c + 1)
                nc.vector.tensor_tensor(wup_lo[:, c, CW:2 * CW], wup_raw[:, c, CW:2 * CW],
                                        wup_hi[:, c, CW:2 * CW].bitcast(F32), ALU.subtract).then_inc(s_uplo_v, 1)

            row_max(0, 0)
            row_max(0, 1)
            up_lo(0)

            def body(b, par, pair, first, last):
                row_max(b, 2)
                row_max(b, 3)
                if first:
                    for c in range(1, CH):
                        up_lo(c)
                invert_sum(b, 0)
                invert_sum(b, 1)
                router_after_exp(b)
                invert_sum(b, 2)
                invert_sum(b, 3)
                for t in range(NT):
                    if t == NT - 1 and not last:
                        row_max(b + 1, 0)
                        row_max(b + 1, 1)
                    if t == 6 and not last:
                        dve.wait_ge(s_st, b + 2)
                    product(b, par, t)
                    if not first or t >= WB_LAG:
                        weighted(b, par, t - WB_LAG)
                    if t == 6 and not last:
                        moments(b + 1)
                    if 3 <= t <= 6:
                        lo_of_probs(b, t - 3)
                    if t == 7 and not first:
                        result(b - 1, 1 - par, pair - 1)
                    if not last:
                        if t == 5:
                            statistics(1 - par, pair)
                        if t == 7:
                            normalise(b + 1, 1 - par)
                        if t == 8:
                            lo_of_x(b + 1, 1 - par)
                        if t == 9:
                            lo_of_kq(b + 1)
                        if t == 10:
                            lo_of_v_and_logits(b + 1)
                        if t == 11:
                            router_before_exp(b + 1)

            bodies(dve, body)
            for t in range(NT, NT + WB_LAG):
                weighted(B - 1, (B - 1) % 2, t - WB_LAG)
            result(B - 1, (B - 1) % 2, (B - 1) // 2)

        @block.tensor
        def _(pe):
            def three(out_ap, w_hi, w_lo, m_hi, m_lo, start=True, stop=True):
                nc.tensor.matmul(out_ap, w_hi, m_hi, start=start, stop=False, skip_group_check=True)
                nc.tensor.matmul(out_ap, w_hi, m_lo, start=False, stop=False, skip_group_check=True)
                return nc.tensor.matmul(out_ap, w_lo, m_hi, start=False, stop=stop, skip_group_check=True)

            def turn_x(b):
                pe.wait_ge(s_xn, b + 1)
                if isinstance(b, int) and b == 0:
                    pe.wait_ge(s_cst, 16)
                for j in range(TJ):
                    ins = nc.tensor.transpose(att[:, 0, j * P:(j + 1) * P], xn[:, j * D:(j + 1) * D], ident)
                ins.then_inc(s_xt, 1)

            def keys_queries(b, par):
                pe.wait_ge(s_xlo, b + 1)
                m = xT_hi[:, par], xT_lo[:, par]
                three(att[:, 1], wq_hi[:, D:2 * D], wq_lo[:, D:2 * D], *m).then_inc(s_k, 1)
                three(att[:, 0], wq_hi[:, 0:D], wq_lo[:, 0:D], *m).then_inc(s_q, 1)

            def values_logits(b, par):
                pe.wait_ge(s_klo, b + 1)
                pe.wait_ge(s_qlo, b + 1)
                wv = slice(2 * D, 2 * D + VG)
                for j in range(TJ):
                    o = att[:, j // 2, (j % 2) * VG:(j % 2 + 1) * VG]
                    cols = slice(j * P, (j + 1) * P)
                    ins = three(o, xT_hi[:, par, cols], xT_lo[:, par, cols], wq_hi[:, wv], wq_lo[:, wv])
                ins.then_inc(s_v, 1)

            def scores(b, j):
                if j == 0:
                    pe.wait_ge(s_vlo, b + 1)
                if j >= 2:
                    pe.wait_ge(s_exp, b * TJ + j - 1)
                q = slice(j * P, (j + 1) * P)
                three(att[:, j % 2], qT_hi[:, q], qT_lo[:, q], kT_hi[:], kT_lo[:]).then_inc(s_sc, 1)

            def turn_probs(b, j):
                pe.wait_ge(s_pn, b * TJ + j + 1)
                if j == 0:
                    pe.wait_ge(s_exp, (b + 1) * TJ)
                elif j == 1:
                    pe.wait_ge(s_wsh, b + 1)
                else:
                    pe.wait_ge(s_ptlo, b * TJ + j - 1)
                for s in range(TJ):
                    ins = nc.tensor.transpose(att[:, (j + 1) % 2, s * P:(s + 1) * P], probs[:, j, s * P:(s + 1) * P], ident)
                ins.then_inc(s_pt, 1)

            def attend(b):
                pe.wait_ge(s_ptlo, (b + 1) * TJ)
                for s in range(TJ):
                    ins = three(acc[:], v_hi[:, s], v_lo[:, s], pT_hi[:, s], pT_lo[:, s], start=False, stop=False)
                ins.then_inc(s_av, 1)

            def turn_weights(b):
                pe.wait_ge(s_gate, (b + 1) * GATE_STEPS)
                pe.wait_ge(s_exp, b * TJ + 3)
                for j in range(TJ):
                    ins = nc.tensor.transpose(att[0:2 * R, 0, j * P:(j + 1) * P], wsplit[:, j].bitcast(F32), ident)
                ins.then_inc(s_wt, 1)

            def turn_result(b):
                pe.wait_ge(s_accs, b + 1)
                for j in range(TJ):
                    ins = nc.tensor.transpose(att[:, 1, j * P:(j + 1) * P], accT[:, j * P:(j + 1) * P], ident)
                ins.then_inc(s_ot, 1)

            def gate_up(b, par, t, first):
                M, n, g = ROWS[t], tile(b, t), 2 * ring(par, t, 2)
                c, cols = divmod(t * P, CW)
                m = xT_hi[:, par], xT_lo[:, par]
                if first:
                    need = -(-min((t + 1) * P, HID) // CW)
                    pe.wait_ge(s_uplo, need)
                    pe.wait_ge(s_uplo_v, need)
                if not (first and t < 2):
                    pe.wait_ge(s_b, n - 1)
                for which, ready in ((0, s_g), (1, s_u)):
                    o = gu[0:M, g + which]
                    whi, wlo = up_columns(t, which)
                    three(o, whi, wlo, *m).then_inc(ready, 1)

            def up_columns(t, which):
                c0 = (2 * t + which) * P - (which * (P - ROWS[t]))
                return (wup_hi[:].rearrange("p c n -> p (c n)")[:, c0:c0 + ROWS[t]],
                        wup_lo[:].rearrange("p c n -> p (c n)")[:, c0:c0 + ROWS[t]])

            def weight_rows(b, par, first):
                pe.wait_ge(s_wts, b + 1)
                if first:
                    pe.wait_ge(s_selr, 1)
                else:
                    pe.wait_ge(s_c, tile(b, ET - NT))
                nc.tensor.matmul(wrow[:], sel[:, 0:P], wT[:, par], start=True, stop=True).then_inc(s_wb, 1)
                nc.tensor.matmul(att[:, 0], sel[:, P:2 * P], wT[:, par], start=True, stop=True).then_inc(s_ws, 1)

            def down(b, par, t):
                M, tt = ROWS[t % NT], t % NT
                slot = ring(par, t, RING)
                if tt == 0 and not (isinstance(b, int) and b == 0):
                    pe.wait_ge(s_accs, b)
                pe.wait_ge(s_hlo, tile(b, t) + 1)
                cols = slice(tt * D, (tt + 1) * D)
                three(acc[:], wdn_hi[0:M, cols], wdn_lo[0:M, cols], h_hi[0:M, slot], h_lo[0:M, slot],
                      start=(tt == 0), stop=(tt == NT - 1)).then_inc(s_d, 1)

            turn_x(0)
            pe.wait_ge(s_wqlo, 1)
            keys_queries(0, 0)
            values_logits(0, 0)
            scores(0, 0)
            scores(0, 1)

            def body(b, par, pair, first, last):
                for t in range(NT):
                    if t == NT - 1 and not last:
                        scores(b + 1, 0)
                        scores(b + 1, 1)
                    gate_up(b, par, t, first)
                    if t == WB_LAG:
                        weight_rows(b, par, first)
                    if t == 0:
                        scores(b, 2)
                        scores(b, 3)
                    if t == 2:
                        turn_weights(b)
                    if 3 <= t <= 6:
                        turn_probs(b, t - 3)
                    if first and t == DOWN_LAG:
                        pe.wait_ge(s_dnlo, 2)
                    if not first or t >= DOWN_LAG:
                        down(b, par, t - DOWN_LAG)
                    if t == 7:
                        if not first:
                            pe.wait_ge(s_ptlo, b * TJ + 3)
                            turn_result(b - 1)
                        attend(b)
                    if not last:
                        if t == 8:
                            turn_x(b + 1)
                        if t == 9:
                            if not first:
                                pe.wait_ge(s_out, b)
                            keys_queries(b + 1, 1 - par)
                        if t == 10:
                            values_logits(b + 1, 1 - par)

            bodies(pe, body)
            b, par = B - 1, (B - 1) % 2
            for t in range(NT, NT + DOWN_LAG):
                down(b, par, t - DOWN_LAG)
            turn_result(b)


_INS = ["x", "w_qkvr", "biases", "w_up", "w_down", "consts", "select"]


def kernel(**inputs):
    import numpy as _np
    import concourse.bacc as _bacc
    from concourse import mybir as _mybir
    from concourse.bass_utils import run_bass_kernel_spmd as _run

    a = {k.replace("L0_attn_", "").replace("L0_ffn_", "f_"): _np.asarray(v) for k, v in inputs.items()}
    f32 = _np.float32
    pad = _np.zeros((D, 1), f32)
    w_qkvr = _np.concatenate([a["Wq"], a["Wk"], a["Wv"], a["f_gate_w"].T, a["f_shared_expert_gate_w"].T, pad], axis=1)
    biases = _np.stack([a["bq"], a["bk"], a["bv"]], axis=1)
    gu = a["f_experts_gate_up"]
    def by_tile(m):
        return m.reshape(E, ET, PE_ROWS, -1).transpose(1, 0, 2, 3).reshape(E * I, -1)

    gate = _np.concatenate([by_tile(gu[:, :I]), a["f_shared_gate_w"]]).T
    up = _np.concatenate([by_tile(gu[:, I:]), a["f_shared_up_w"]]).T
    w_up = _np.concatenate([m[:, t * P:t * P + ROWS[t]] for t in range(NT) for m in (gate, up)], axis=1)
    w_up = w_up.reshape(P, CH, 2 * CW)
    down = _np.concatenate([by_tile(a["f_experts_down"].transpose(0, 2, 1)), a["f_shared_down_w"].T,
                            _np.zeros((NT * P - HID, D), f32)])
    w_down = down.reshape(NT, P, D).transpose(1, 0, 2).reshape(P, NT * D)
    tie = _np.zeros((E, E), f32)
    for e in range(E):
        tie[e, :e] = -1.2e-38
    consts = _np.concatenate([_np.eye(P, dtype=f32), _np.tile(tie.reshape(1, E * E), (P, 1))], axis=1)
    select = _np.zeros((2 * R, 2 * P), f32)
    for p in range(P):
        e = p // PE_ROWS
        select[e, p] = select[R + e, p] = 1.0
    select[E, P:] = select[R + E, P:] = 1.0

    arrays = dict(zip(_INS, [a["x"], w_qkvr, biases, w_up, w_down, consts, select]))
    nc = _bacc.Bacc("TRN2", target_bir_lowering=False, num_devices=1)
    feed, args = {}, []
    for name in _INS:
        m = _np.ascontiguousarray(arrays[name])
        feed[f"in_{name}_dram"] = m
        args.append(nc.dram_tensor(f"in_{name}_dram", m.shape, _mybir.dt.from_np(m.dtype), kind="ExternalInput").ap())
    out = nc.dram_tensor("out_dram", (B, S, D), F32, kind="ExternalOutput").ap()
    moe_attention_layer(nc, *args, out)
    return _run(nc, [feed], core_ids=[0]).results[0]["out_dram"]
```

```python
from contextlib import ExitStack

import concourse.bass as bass
from concourse import mybir

F32 = mybir.dt.float32
F32R = mybir.dt.float32r
ALU = mybir.AluOpType
ACT = mybir.ActivationFunctionType
AX = mybir.AxisListType

P = 128
B, S, D = 8, 512, 128
TJ = S // P
E, I, SI = 8, 176, 352
K_TOP = 2
R = E + 1
HID = E * I + SI
PE_ROWS = P // E
ET = I // PE_ROWS
NT = -(-HID // P)
ROWS = [min(P, HID - P * t) for t in range(NT)]
CH = 4
CW = HID // CH
DW = NT * D // 2
VG = D + R + 1
QKV = 2 * D + VG
SCALE = 1.0 / float(D) ** 0.5
EPS = 1e-5
WB_LAG, HID_LAG, DOWN_LAG = 3, 4, 6
HOLD = 2
WARM_UP = 12
RING = 7
HID_RING = 4
GATE_STEPS = 12


def moe_attention_layer(nc, x, x_t, front, w_up, w_down, select, out_t):
    x_v = x.rearrange("b (p j) d -> b p (j d)", j=TJ)

    with ExitStack() as ctx:
        def sb(name, shape, dt=F32):
            return ctx.enter_context(nc.sbuf_tensor(name, shape, dt))

        def pb(name, shape):
            return ctx.enter_context(nc.psum_tensor(name, shape, F32))

        def sem(name):
            return ctx.enter_context(nc.semaphore(name))

        frt = sb("frt", [P, QKV + 3 + P + E * E])
        wq_raw = frt[:, 0:QKV]
        bias = frt[:, QKV:QKV + 3]
        ident = frt[:, QKV + 3:QKV + 3 + P]
        tie = frt[:, QKV + 3 + P:QKV + 3 + P + E * E]
        wqs = sb("wqs", [P, D])
        bqs = sb("bqs", [P, 1])
        wup_raw = sb("wup_raw", [P, CH, 2 * CW])
        wdn_raw = sb("wdn_raw", [P, NT * D])
        sel_raw = sb("sel_raw", [2 * R, 2 * P])
        wq_hi, wq_lo = sb("wq_hi", [P, QKV], F32R), sb("wq_lo", [P, QKV], F32R)
        wup_hi, wup_lo = sb("wup_hi", [P, CH, 2 * CW], F32R), sb("wup_lo", [P, CH, 2 * CW], F32R)
        wdn_hi, wdn_lo = sb("wdn_hi", [P, NT * D], F32R), sb("wdn_lo", [P, NT * D], F32R)
        sel = sb("sel", [2 * R, 2 * P], F32R)
        mhalf = sb("mhalf", [P, TJ])
        ones = sb("ones", [P, S], mybir.dt.bfloat16)

        xs = sb("xs", [P, 2, S])
        xr = sb("xr", [P, 2, S])
        stats = sb("stats", [P, TJ, 6])
        mv = sb("mv", [P, TJ, 2])
        veps = sb("veps", [P, TJ])
        rstd = sb("rstd", [P, TJ])
        xn = sb("xn", [P, S])
        xT_hi, xT_lo = sb("xT_hi", [P, 2, S], F32R), sb("xT_lo", [P, 2, S], F32R)
        kT_hi, kT_lo = sb("kT_hi", [P, S], F32R), sb("kT_lo", [P, S], F32R)
        qT_hi, qT_lo = sb("qT_hi", [P, S], F32R), sb("qT_lo", [P, S], F32R)
        v_hi, v_lo = sb("v_hi", [P, 2, TJ, D], F32R), sb("v_lo", [P, 2, TJ, D], F32R)
        probs = sb("probs", [P, TJ, S])
        nmax = sb("nmax", [P, TJ])
        psums = sb("psums", [P, TJ])
        pinv = sb("pinv", [P, TJ])
        pT_hi, pT_lo = sb("pT_hi", [P, TJ, S], F32R), sb("pT_lo", [P, TJ, S], F32R)
        logit = sb("logit", [P, TJ, R])
        diff = sb("diff", [P, TJ, E, E])
        beats = sb("beats", [P, TJ, E, E])
        rank = sb("rank", [P, TJ, E])
        lmax = sb("lmax", [P, TJ])
        ein = sb("ein", [P, TJ, R])
        eout = sb("eout", [P, TJ, R])
        den = sb("den", [P, TJ, 2])
        rden = sb("rden", [P, TJ, 2])
        wtop = sb("wtop", [P, TJ, E])
        wts = sb("wts", [P, TJ, R])
        wsplit = sb("wsplit", [P, TJ, 2 * R], F32R)
        wT = sb("wT", [2 * R, S], F32R)
        wshared = sb("wshared", [P, S])
        silu = sb("silu", [P, 2, S])
        prod = sb("prod", [P, RING, S])
        hid = sb("hid", [P, HID_RING, S])
        h_hi, h_lo = sb("h_hi", [P, RING, S], F32R), sb("h_lo", [P, RING, S], F32R)
        res = sb("res", [P, S])

        att = pb("att", [P, 2, S])
        gu = pb("gu", [P, 4, S])
        wrow = pb("wrow", [P, S])
        acc = pb("acc", [P, S])

        s_front, s_dn, s_sel, s_store = map(sem, ["front_loaded", "down_loaded", "select_loaded", "stored"])
        s_x = [sem("x_even_loaded"), sem("x_odd_loaded")]
        s_x0 = sem("x_first_half_loaded")
        s_r = [sem("residual_even_loaded"), sem("residual_odd_loaded")]
        s_up = [sem(f"up_loaded{c}") for c in range(CH)]
        s_wqs, s_mhalf, s_ones = sem("q_scaled"), sem("mhalf_set"), sem("ones_set")
        s_wqhi, s_wqlo = sem("qkv_hi"), sem("qkv_lo")
        s_uphi, s_uplo_1, s_uplo_2 = sem("up_hi"), sem("up_lo_first_half"), sem("up_lo_second_half")
        s_dnhi, s_dnlo, s_selr = sem("down_hi"), sem("down_lo"), sem("select_rounded")
        s_xt, s_k, s_q, s_v, s_sc, s_pt, s_wt = map(
            sem, ["xT_made", "k_made", "q_made", "v_made", "scores_made", "pT_made",
                  "wT_made"])
        s_g, s_u, s_wb, s_ws, s_d = map(sem, ["gate_made", "up_made", "wrow_made", "shared_row_made", "down_made"])
        s_gexp, s_exp, s_silu, s_xhi, s_khi, s_qhi, s_vhi, s_wts, s_pthi, s_hhi = map(
            sem, ["router_exp", "probs_exp", "silu_made", "xT_hi_made", "k_hi_made", "q_hi_made",
                  "v_hi_made", "wT_kept", "pT_hi_made", "h_hi_made"])
        s_wsh = sem("shared_weight_kept")
        s_st, s_mv, s_ve, s_xn, s_xlo, s_klo, s_qlo, s_vlo, s_gate, s_split, s_max, s_pinv, s_ptlo, \
            s_b, s_c, s_hlo_last, s_out = map(
                sem, ["stats_made", "moments_made", "var_eps", "xn_made", "xT_lo_made", "k_lo_made",
                      "q_lo_made", "v_lo_made", "router_step", "weights_hi", "max_made", "sum_inverted",
                      "pT_lo_made", "prod_made", "hid_made", "last_h_lo_made", "result_made"])
        s_rstd, s_pn, s_hlo = sem("rstd_made"), sem("probs_scaled"), sem("h_lo_made")

        def tile(b, t):
            return b * NT + t

        def scores_bank(b, j):
            if j < 2:
                return att[:, j]
            if isinstance(b, int) and b == 0:
                return (wrow[:], acc[:])[j - 2]
            return gu[:, j]

        def ring(par, t, size):
            return (NT * par + t) % size

        def due(t, lag, first, last, hold=0):
            def done(t):
                if last and t > NT - 5:
                    return t - lag + 1 + min(2, t - NT + 5)
                if t < 0 or t >= NT - hold:
                    t = (-1 if t < 0 else NT - 1) - hold
                if hold and t == lag:
                    t = lag - 1
                return t - lag + 1
            return range(max(done(t - 1), 0 if first else -NT), done(t))

        def rest(lag):
            return range(NT - lag + 2, NT)

        def bodies(eng, body):
            body(0, 0, 0, True, False)
            with eng.Fori(0, (B - 2) // 2) as i:
                body(i * 2 + 1, 1, i + 1, False, False)
                body(i * 2 + 2, 0, i + 1, False, False)
            body(B - 1, (B - 1) % 2, B // 2, False, True)

        block = ctx.enter_context(nc.Block())

        @block.sync
        def _(sp):
            sp.dma_start(xs[:, 0, 0:S // 2], x_v[0, :, 0:S // 2]).then_inc(s_x0, 16)
            sp.dma_start(xs[:, 0, S // 2:S], x_v[0, :, S // 2:S]).then_inc(s_x[0], 16)
            sp.dma_start(frt[:], front).then_inc(s_front, 16)
            for c in range(CH):
                sp.dma_start(wup_raw[:, c], w_up[:, c]).then_inc(s_up[c], 16)
            sp.dma_start(sel_raw[:], select).then_inc(s_sel, 16)
            sp.dma_start(wdn_raw[:], w_down).then_inc(s_dn, 16)
            sp.dma_start(xs[:, 1, :], x_v[1]).then_inc(s_x[1], 16)
            for b in range(2):
                sp.dma_start(xr[:, b, :], x_t[b]).then_inc(s_r[b], 16)
            sp.sem_inc(s_store, 16)

            def batch_of(v, b):
                return v[b] if isinstance(b, int) else v[bass.ds(b, 1)].rearrange("a p n -> (a p) n")

            def load_and_store(b, par, more):
                if more:
                    sp.wait_ge(s_xn, (b + 1) * TJ)
                    sp.dma_start(xs[:, par, :], batch_of(x_v, b + 2)).then_inc(s_x[par], 16)
                sp.wait_ge(s_out, b + 1)
                sp.dma_start(batch_of(out_t, b), res[:]).then_inc(s_store, 16)
                if more:
                    sp.dma_start(xr[:, par, :], batch_of(x_t, b + 2)).then_inc(s_r[par], 16)

            with sp.Fori(0, (B - 2) // 2) as i:
                load_and_store(i * 2, 0, True)
                load_and_store(i * 2 + 1, 1, True)
            load_and_store(B - 2, 0, False)
            load_and_store(B - 1, 1, False)
            sp.wait_ge(s_store, 16 * (B + 1))

        @block.gpsimd
        def _(pool):
            nc.gpsimd.memset(ones[:], 1.0).then_inc(s_ones, 1)
            nc.gpsimd.memset(mhalf[:], -0.5).then_inc(s_mhalf, 1)

            def norm(b):
                pool.wait_ge(s_ve, b + 1)
                if isinstance(b, int) and b == 0:
                    pool.wait_ge(s_mhalf, 1)
                nc.gpsimd.tensor_tensor(rstd[:], veps[:], mhalf[:], ALU.pow).then_inc(s_rstd, 1)

            norm(0)

            for c in range(CH):
                pool.wait_ge(s_uphi, c + 1)
                nc.gpsimd.tensor_tensor(wup_lo[:, c, 0:CW], wup_raw[:, c, 0:CW],
                                        wup_hi[:, c, 0:CW].bitcast(F32), ALU.subtract).then_inc(s_uplo_1, 1)

            def down_lo(c):
                pool.wait_ge(s_dnhi, c + 1)
                nc.gpsimd.tensor_tensor(wdn_lo[:, c * DW:(c + 1) * DW], wdn_raw[:, c * DW:(c + 1) * DW],
                                        wdn_hi[:, c * DW:(c + 1) * DW].bitcast(F32), ALU.subtract).then_inc(s_dnlo, 1)

            def hidden_lo(b, par, t):
                M = ROWS[t % NT]
                pool.wait_ge(s_hhi, tile(b, t) + 1)
                nc.gpsimd.tensor_tensor(h_lo[0:M, ring(par, t, RING)], hid[0:M, ring(par, t, HID_RING)],
                                        h_hi[0:M, ring(par, t, RING)].bitcast(F32), ALU.subtract).then_inc(s_hlo, 1)

            def scale_probs(b, j):
                pool.wait_ge(s_pinv, b * TJ + j + 1)
                nc.gpsimd.tensor_tensor(probs[:, j], probs[:, j], pinv[:, j:j + 1].broadcast_to([P, S]),
                                        ALU.mult).then_inc(s_pn, 1)

            def body(b, par, pair, first, last):
                for t in range(NT):
                    if t < TJ:
                        scale_probs(b, t)
                    if first and t in (1, 3):
                        down_lo(t // 2)
                    for h in due(t, HID_LAG, first, last):
                        hidden_lo(b, par, h)
                    if t == 4 and not last:
                        norm(b + 1)

            bodies(pool, body)
            for t in rest(HID_LAG)[:-1]:
                hidden_lo(B - 1, (B - 1) % 2, t)

        @block.scalar
        def _(act):
            def hi_of_x(b, par):
                act.wait_ge(s_xt, b + 1)
                nc.scalar.activation(xT_hi[:, par], att[:, 0], ACT.Copy).then_inc(s_xhi, 1)

            def hi_of_kq(b):
                act.wait_ge(s_k, b + 1)
                nc.scalar.activation(kT_hi[:], att[:, 1], ACT.Identity, bias=bias[:, 1:2]).then_inc(s_khi, 1)
                act.wait_ge(s_q, b + 1)
                nc.scalar.activation(qT_hi[:], att[:, 0], ACT.Identity, bias=bqs[:]).then_inc(s_qhi, 1)

            def hi_of_v(b, par, banks):
                act.wait_ge(s_v, b + 1)
                nc.scalar.activation(v_hi[:, par].rearrange("p (a k) d -> p a k d", a=2),
                                     banks[:, :, 0:2 * VG].rearrange("p a (k c) -> p a k c", k=2)[:, :, :, 0:D],
                                     ACT.Copy).then_inc(s_vhi, 1)

            def weights_kept(b):
                act.wait_ge(s_wt, b + 1)
                nc.scalar.activation(wT[:], att[0:2 * R, 0], ACT.Copy).then_inc(s_wts, 1)

            def shared_weight(b, first):
                act.wait_ge(s_ws, b + 1)
                if not first:
                    act.wait_ge(s_c, tile(b, 0))
                nc.scalar.activation(wshared[:], att[:, 0], ACT.Copy).then_inc(s_wsh, 1)

            def hidden_hi(b, par, t):
                M = ROWS[t % NT]
                act.wait_ge(s_c, tile(b, t) + 1)
                if not (isinstance(b, int) and b == 0 and t < RING):
                    act.wait_ge(s_d, tile(b, t) - RING + 1)
                nc.scalar.activation(h_hi[0:M, ring(par, t, RING)], hid[0:M, ring(par, t, HID_RING)], ACT.Copy).then_inc(s_hhi, 1)

            act.wait_ge(s_wqs, 2)
            nc.scalar.activation(wq_hi[:, 0:D], wqs[:], ACT.Copy)
            nc.scalar.activation(wq_hi[:, D:QKV], wq_raw[:, D:QKV], ACT.Copy).then_inc(s_wqhi, 1)

            def up_hi(c):
                act.wait_ge(s_up[c], 16)
                nc.scalar.activation(wup_hi[:, c], wup_raw[:, c], ACT.Copy).then_inc(s_uphi, 1)

            up_hi(0)
            hi_of_x(0, 0)
            up_hi(1)
            hi_of_kq(0)
            up_hi(2)
            hi_of_v(0, 0, gu[:, 2:4])
            up_hi(3)

            def down_hi(c):
                act.wait_ge(s_dn, 16)
                nc.scalar.activation(wdn_hi[:, c * DW:(c + 1) * DW], wdn_raw[:, c * DW:(c + 1) * DW],
                                     ACT.Copy).then_inc(s_dnhi, 1)

            def select_rounded():
                act.wait_ge(s_sel, 16)
                nc.scalar.activation(sel[:], sel_raw[:], ACT.Copy).then_inc(s_selr, 1)

            def exponentials(b):
                for j in range(TJ):
                    act.wait_ge(s_max, b * TJ + j + 1)
                    nc.scalar.activation(probs[:, j], scores_bank(b, j), ACT.Exp, bias=nmax[:, j:j + 1],
                                         accum_out=psums[:, j:j + 1]).then_inc(s_exp, 1)
                act.wait_ge(s_gate, b * GATE_STEPS + 6)
                nc.scalar.activation(eout[:], ein[:], ACT.Exp).then_inc(s_gexp, 1)

            def body(b, par, pair, first, last):
                for t in range(NT):
                    M = ROWS[t]
                    if t == 0:
                        exponentials(b)
                    act.wait_ge(s_g, tile(b, t) + 1)
                    nc.scalar.activation(silu[0:M, ring(par, t, 2)], gu[0:M, 2 * ring(par, t, 2)],
                                         ACT.Silu).then_inc(s_silu, 1)
                    for h in due(t, HID_LAG, first, last):
                        hidden_hi(b, par, h)
                    if first and t == 1:
                        down_hi(0)
                        select_rounded()
                    if first and t == 2:
                        down_hi(1)
                    if t == 2:
                        weights_kept(b)
                    if t == WB_LAG:
                        shared_weight(b, first)
                    if 3 <= t <= 6:
                        j = t - 3
                        act.wait_ge(s_pt, b * TJ + j + 1)
                        nc.scalar.activation(pT_hi[:, :, j * P:(j + 1) * P],
                                             att[:, (j + 1) % 2].rearrange("p (s q) -> p s q", s=TJ),
                                             ACT.Copy).then_inc(s_pthi, 1)
                    if not last:
                        if t == 8:
                            hi_of_x(b + 1, 1 - par)
                        if t == 9:
                            hi_of_kq(b + 1)
                        if t == 10:
                            hi_of_v(b + 1, 1 - par, att)

            bodies(act, body)
            for t in rest(HID_LAG):
                hidden_hi(B - 1, (B - 1) % 2, t)

        @block.vector
        def _(dve):
            def statistics(par, nth, first=False):
                if first:
                    dve.wait_ge(s_x0, 16)
                for j in range(TJ):
                    if j == (TJ // 2 if first else 0):
                        dve.wait_ge(s_x[par], (nth + 1) * 16)
                    ins = nc.vector.bn_stats(stats[:, j], xs[:, par, j * D:(j + 1) * D])
                ins.then_inc(s_st, 1)

            def moments(b):
                for j in range(TJ):
                    ins = nc.vector.bn_aggr(mv[:, j], stats[:, j])
                ins.then_inc(s_mv, 1)
                dve.wait_ge(s_mv, b + 1)
                nc.vector.tensor_scalar(veps[:], mv[:, :, 1], EPS, None, ALU.add).then_inc(s_ve, 1)

            def normalise(b, par):
                dve.wait_ge(s_rstd, b + 1)
                for j in range(TJ):
                    nc.vector.tensor_scalar(xn[:, j * D:(j + 1) * D], xs[:, par, j * D:(j + 1) * D],
                                            mv[:, j, 0:1], rstd[:, j:j + 1], ALU.subtract, ALU.mult).then_inc(s_xn, 1)

            def lo_of_x(b, par):
                dve.wait_ge(s_xhi, b + 1)
                nc.vector.tensor_tensor(xT_lo[:, par], att[:, 0], xT_hi[:, par].bitcast(F32),
                                        ALU.subtract).then_inc(s_xlo, 1)

            def lo_of_kq(b):
                dve.wait_ge(s_khi, b + 1)
                nc.vector.scalar_tensor_tensor(out=kT_lo[:], in0=att[:, 1], scalar=bias[:, 1:2], in1=kT_hi[:].bitcast(F32),
                                               op0=ALU.add, op1=ALU.subtract).then_inc(s_klo, 1)
                dve.wait_ge(s_qhi, b + 1)
                nc.vector.scalar_tensor_tensor(out=qT_lo[:], in0=att[:, 0], scalar=bqs[:], in1=qT_hi[:].bitcast(F32),
                                               op0=ALU.add, op1=ALU.subtract).then_inc(s_qlo, 1)

            def lo_of_v_and_logits(b, par, banks):
                va = banks[:, :, 0:2 * VG].rearrange("p a (k c) -> p a k c", k=2)
                dve.wait_ge(s_vhi, b + 1)
                nc.vector.tensor_copy(logit[:].rearrange("p (a k) r -> p a k r", a=2),
                                      va[:, :, :, D:D + R]).then_inc(s_gate, 1)
                nc.vector.tensor_tensor(v_lo[:, par].rearrange("p (a k) d -> p a k d", a=2), va[:, :, :, 0:D],
                                        v_hi[:, par].bitcast(F32).rearrange("p (a k) d -> p a k d", a=2),
                                        ALU.subtract).then_inc(s_vlo, 1)

            def router_before_exp(b):
                def step(k):
                    dve.wait_ge(s_gate, b * GATE_STEPS + k)

                step(1)
                le = logit[:, :, 0:E]
                nc.vector.tensor_reduce(lmax[:], le, AX.X, ALU.max).then_inc(s_gate, 1)
                nc.vector.tensor_tensor(diff[:], le.unsqueeze(2).broadcast_to([P, TJ, E, E]),
                                        le.unsqueeze(3).broadcast_to([P, TJ, E, E]), ALU.subtract).then_inc(s_gate, 1)
                step(2)
                nc.vector.tensor_tensor(ein[:, :, 0:E], le, lmax[:].unsqueeze(2).broadcast_to([P, TJ, E]),
                                        ALU.subtract).then_inc(s_gate, 1)
                step(3)
                nc.vector.tensor_tensor(beats[:], diff[:],
                                        tie.rearrange("p (a c) -> p a c", a=E).unsqueeze(1).broadcast_to([P, TJ, E, E]),
                                        ALU.is_gt).then_inc(s_gate, 1)
                nc.vector.tensor_scalar(ein[:, :, E:R], logit[:, :, E:R], -1.0, 87.0, ALU.mult, ALU.min).then_inc(s_gate, 1)

            def router_after_exp(b):
                def step(k):
                    dve.wait_ge(s_gate, b * GATE_STEPS + k)

                step(5)
                nc.vector.tensor_reduce(rank[:], beats[:], AX.X, ALU.add).then_inc(s_gate, 1)
                dve.wait_ge(s_gexp, b + 1)
                nc.vector.tensor_reduce(den[:, :, 0:1], eout[:, :, 0:E], AX.X, ALU.add)
                nc.vector.tensor_scalar(den[:, :, 1:2], eout[:, :, E:R], 1.0, None, ALU.add).then_inc(s_gate, 1)
                step(7)
                nc.vector.scalar_tensor_tensor(out=wtop[:], in0=rank[:], scalar=float(K_TOP), in1=eout[:, :, 0:E],
                                               op0=ALU.is_lt, op1=ALU.mult).then_inc(s_gate, 1)
                step(8)
                nc.vector.reciprocal(rden[:], den[:]).then_inc(s_gate, 1)
                step(10)
                nc.vector.tensor_tensor(wts[:, :, 0:E], wtop[:], rden[:, :, 0:1].broadcast_to([P, TJ, E]), ALU.mult)
                nc.vector.tensor_copy(wts[:, :, E:R], rden[:, :, 1:2]).then_inc(s_gate, 1)
                step(11)
                nc.vector.tensor_copy(wsplit[:, :, 0:R], wts[:]).then_inc(s_split, 1)
                dve.wait_ge(s_split, b + 1)
                nc.vector.tensor_tensor(wsplit[:, :, R:2 * R], wts[:], wsplit[:, :, 0:R].bitcast(F32),
                                        ALU.subtract).then_inc(s_gate, 1)

            def row_max(b, j):
                dve.wait_ge(s_sc, b * TJ + j + 1)
                nc.vector.tensor_reduce(nmax[:, j:j + 1], scores_bank(b, j), AX.X, ALU.max, negate=True).then_inc(s_max, 1)

            def invert_sum(b, j):
                dve.wait_ge(s_exp, b * TJ + j + 1)
                nc.vector.reciprocal(pinv[:, j:j + 1], psums[:, j:j + 1]).then_inc(s_pinv, 1)

            def lo_of_probs(b, j):
                dve.wait_ge(s_pthi, b * TJ + j + 1)
                nc.vector.tensor_tensor(pT_lo[:, :, j * P:(j + 1) * P],
                                        att[:, (j + 1) % 2].rearrange("p (s q) -> p s q", s=TJ),
                                        pT_hi[:, :, j * P:(j + 1) * P].bitcast(F32), ALU.subtract).then_inc(s_ptlo, 1)

            def product(b, par, t):
                M = ROWS[t]
                dve.wait_ge(s_silu, tile(b, t) + 1)
                dve.wait_ge(s_u, tile(b, t) + 1)
                nc.vector.tensor_tensor(prod[0:M, ring(par, t, RING)], silu[0:M, ring(par, t, 2)],
                                        gu[0:M, 2 * ring(par, t, 2) + 1], ALU.mult).then_inc(s_b, 1)

            def weighted(b, par, t):
                M = ROWS[t % NT]
                n = tile(b, t)
                if t == 0:
                    dve.wait_ge(s_wb, b + 1)
                if t % NT == ET:
                    dve.wait_ge(s_wsh, b + 1 if t > 0 else b)
                dve.wait_ge(s_b, n + 1)
                if not (isinstance(b, int) and b == 0 and t < HID_RING):
                    dve.wait_ge(s_hlo, n - HID_RING + 1)
                nc.vector.tensor_tensor(hid[0:M, ring(par, t, HID_RING)], prod[0:M, ring(par, t, RING)],
                                        (wrow if t % NT < ET else wshared)[0:M, :],
                                        ALU.mult).then_inc(s_c, 1)

            def result(b, par, nth):
                dve.wait_ge(s_d, tile(b, NT))
                dve.wait_ge(s_r[par], (nth + 1) * 16)
                dve.wait_ge(s_store, (b + 1) * 16)
                nc.vector.scalar_tensor_tensor(out=res[:], in0=acc[:], scalar=bias[:, 2:3], in1=xr[:, par],
                                               op0=ALU.add, op1=ALU.add).then_inc(s_out, 1)

            statistics(0, 0, first=True)
            dve.wait_ge(s_st, 1)
            moments(0)
            dve.wait_ge(s_front, 16)
            nc.vector.tensor_scalar(wqs[:], wq_raw[:, 0:D], SCALE, None, ALU.mult).then_inc(s_wqs, 1)
            nc.vector.tensor_scalar(bqs[:], bias[:, 0:1], SCALE, None, ALU.mult).then_inc(s_wqs, 1)
            normalise(0, 0)
            dve.wait_ge(s_wqhi, 1)
            dve.wait_ge(s_wqs, 1)
            nc.vector.tensor_tensor(wq_lo[:, 0:D], wqs[:], wq_hi[:, 0:D].bitcast(F32), ALU.subtract)
            nc.vector.tensor_tensor(wq_lo[:, D:QKV], wq_raw[:, D:QKV],
                                    wq_hi[:, D:QKV].bitcast(F32), ALU.subtract).then_inc(s_wqlo, 1)
            lo_of_x(0, 0)

            def up_lo(c):
                dve.wait_ge(s_uphi, c + 1)
                nc.vector.tensor_tensor(wup_lo[:, c, CW:2 * CW], wup_raw[:, c, CW:2 * CW],
                                        wup_hi[:, c, CW:2 * CW].bitcast(F32), ALU.subtract).then_inc(s_uplo_2, 1)

            up_lo(0)
            lo_of_kq(0)
            lo_of_v_and_logits(0, 0, gu[:, 2:4])
            row_max(0, 0)
            row_max(0, 1)
            row_max(0, 2)
            row_max(0, 3)
            router_before_exp(0)

            def body(b, par, pair, first, last):
                for t in range(NT):
                    if t == 0:
                        if not first:
                            row_max(b, 2)
                            row_max(b, 3)
                        invert_sum(b, 0)
                        invert_sum(b, 1)
                        router_after_exp(b)
                        invert_sum(b, 2)
                        invert_sum(b, 3)
                    if t == NT - 1 and not last:
                        row_max(b + 1, 0)
                        row_max(b + 1, 1)
                    if t == 4 and not last:
                        dve.wait_ge(s_st, b + 2)
                    product(b, par, t)
                    if first and 1 <= t < CH:
                        up_lo(t)
                    for h in due(t, WB_LAG, first, last):
                        weighted(b, par, h)
                    if t == DOWN_LAG - 1 and not first:
                        result(b - 1, 1 - par, pair - 1)
                    if t == 4 and not last:
                        moments(b + 1)
                    if 3 <= t <= 6:
                        lo_of_probs(b, t - 3)
                    if not last:
                        if t == 3:
                            statistics(1 - par, pair)
                        if t == 6:
                            normalise(b + 1, 1 - par)
                        if t == 8:
                            lo_of_x(b + 1, 1 - par)
                        if t == 9:
                            lo_of_kq(b + 1)
                        if t == 10:
                            lo_of_v_and_logits(b + 1, 1 - par, att)
                        if t == 11:
                            router_before_exp(b + 1)

            bodies(dve, body)
            b, par = B - 1, (B - 1) % 2
            for t in rest(WB_LAG):
                weighted(b, par, t)
            t, M = NT - 1, ROWS[NT - 1]
            dve.wait_ge(s_hhi, tile(b, t) + 1)
            nc.vector.tensor_tensor(h_lo[0:M, ring(par, t, RING)], hid[0:M, ring(par, t, HID_RING)],
                                    h_hi[0:M, ring(par, t, RING)].bitcast(F32), ALU.subtract).then_inc(s_hlo_last, 1)
            result(b, par, (B - 1) // 2)

        @block.tensor
        def _(pe):
            def three(out_ap, w_hi, w_lo, m_hi, m_lo, start=True, stop=True, m_lo_made=None):
                nc.tensor.matmul(out_ap, w_lo, m_hi, start=start, stop=False, skip_group_check=True)
                nc.tensor.matmul(out_ap, w_hi, m_hi, start=False, stop=False, skip_group_check=True)
                if m_lo_made:
                    pe.wait_ge(*m_lo_made)
                return nc.tensor.matmul(out_ap, w_hi, m_lo, start=False, stop=stop, skip_group_check=True)

            def turn_x(b):
                if isinstance(b, int) and b == 0:
                    pe.wait_ge(s_front, 16)
                for j in range(TJ):
                    pe.wait_ge(s_xn, b * TJ + j + 1)
                    ins = nc.tensor.transpose(att[:, 0, j * P:(j + 1) * P], xn[:, j * D:(j + 1) * D], ident)
                ins.then_inc(s_xt, 1)

            def keys_queries(b, par):
                pe.wait_ge(s_xhi, b + 1)
                m = xT_hi[:, par], xT_lo[:, par]
                three(att[:, 1], wq_hi[:, D:2 * D], wq_lo[:, D:2 * D], *m, m_lo_made=(s_xlo, b + 1)).then_inc(s_k, 1)
                three(att[:, 0], wq_hi[:, 0:D], wq_lo[:, 0:D], *m).then_inc(s_q, 1)

            def values_logits(b, par, banks):
                wv = slice(2 * D, 2 * D + VG)
                for j in range(TJ):
                    o = banks[:, j // 2, (j % 2) * VG:(j % 2 + 1) * VG]
                    cols = slice(j * P, (j + 1) * P)
                    ins = three(o, xT_hi[:, par, cols], xT_lo[:, par, cols], wq_hi[:, wv], wq_lo[:, wv])
                ins.then_inc(s_v, 1)

            def scores(b, j):
                if j == 2 and not (isinstance(b, int) and b == 0):
                    pe.wait_ge(s_b, tile(b, 0))
                if j == 0 and isinstance(b, int) and b == 0:
                    pe.wait_ge(s_klo, 1)
                    pe.wait_ge(s_qlo, 1)
                elif j == 0:
                    pe.wait_ge(s_vlo, b + 1)
                q = slice(j * P, (j + 1) * P)
                three(scores_bank(b, j), qT_hi[:, q], qT_lo[:, q], kT_hi[:], kT_lo[:]).then_inc(s_sc, 1)

            def turn_probs(b, j):
                pe.wait_ge(s_pn, b * TJ + j + 1)
                if j == 1:
                    pe.wait_ge(s_wsh, b + 1)
                elif j > 1:
                    pe.wait_ge(s_ptlo, b * TJ + j - 1)
                for s in range(TJ):
                    ins = nc.tensor.transpose(att[:, (j + 1) % 2, s * P:(s + 1) * P], probs[:, j, s * P:(s + 1) * P], ident)
                ins.then_inc(s_pt, 1)

            def attend(b, par, blocks):
                if 0 in blocks:
                    pe.wait_ge(s_ptlo, (b + 1) * TJ)
                for s in blocks:
                    three(acc[:], v_hi[:, par, s], v_lo[:, par, s], pT_hi[:, s], pT_lo[:, s], start=False, stop=False)

            def turn_weights(b):
                pe.wait_ge(s_gate, (b + 1) * GATE_STEPS)
                for j in range(TJ):
                    ins = nc.tensor.transpose(att[0:2 * R, 0, j * P:(j + 1) * P], wsplit[:, j].bitcast(F32), ident)
                ins.then_inc(s_wt, 1)

            def gate_up(b, par, t, first):
                M, n, g = ROWS[t], tile(b, t), 2 * ring(par, t, 2)
                m = xT_hi[:, par], xT_lo[:, par]
                if first:
                    need = -(-min((t + 1) * P, HID) // CW)
                    pe.wait_ge(s_uplo_1, need)
                    pe.wait_ge(s_uplo_2, need)
                if not (first and t < 2):
                    pe.wait_ge(s_b, n - 1)
                for which, ready in ((0, s_g), (1, s_u)):
                    o = gu[0:M, g + which]
                    whi, wlo = up_columns(t, which)
                    three(o, whi, wlo, *m).then_inc(ready, 1)

            def up_columns(t, which):
                c0 = (2 * t + which) * P - (which * (P - ROWS[t]))
                return (wup_hi[:].rearrange("p c n -> p (c n)")[:, c0:c0 + ROWS[t]],
                        wup_lo[:].rearrange("p c n -> p (c n)")[:, c0:c0 + ROWS[t]])

            def weight_rows(b, first):
                pe.wait_ge(s_wts, b + 1)
                if first:
                    pe.wait_ge(s_selr, 1)
                    pe.wait_ge(s_exp, TJ)
                else:
                    pe.wait_ge(s_c, tile(b, ET - NT))
                nc.tensor.matmul(wrow[:], sel[:, 0:P], wT[:], start=True, stop=True).then_inc(s_wb, 1)
                nc.tensor.matmul(att[:, 0], sel[:, P:2 * P], wT[:], start=True, stop=True).then_inc(s_ws, 1)

            def down(b, par, t):
                M, tt = ROWS[t % NT], t % NT
                slot = ring(par, t, RING)
                if tt == 0 and isinstance(b, int) and b == 0:
                    pe.wait_ge(s_dnlo, 2)
                elif tt == 0:
                    pe.wait_ge(s_out, b)
                pe.wait_ge(s_hhi, tile(b, t) + 1)
                if isinstance(b, int) and b == B - 1 and t == NT - 1:
                    lo_made = s_hlo_last, 1
                else:
                    lo_made = s_hlo, tile(b, t) + 1
                cols = slice(tt * D, (tt + 1) * D)
                three(acc[:], wdn_hi[0:M, cols], wdn_lo[0:M, cols], h_hi[0:M, slot], h_lo[0:M, slot],
                      start=(tt == 0), stop=(tt == NT - 1), m_lo_made=lo_made).then_inc(s_d, 1)

            pe.wait_ge(s_ones, 1)
            for _ in range(WARM_UP):
                nc.tensor.matmul(acc[:], ones[:, 0:P], ones[:], start=True, stop=True)

            turn_x(0)
            pe.wait_ge(s_wqlo, 1)
            keys_queries(0, 0)
            values_logits(0, 0, gu[:, 2:4])
            for j in range(TJ):
                scores(0, j)

            def body(b, par, pair, first, last):
                for t in range(NT):
                    if t == NT - 1 and not last:
                        scores(b + 1, 0)
                        scores(b + 1, 1)
                    if t == 1 and first:
                        pe.wait_ge(s_vlo, 1)
                    elif t == 1:
                        pe.wait_ge(s_exp, (b + 1) * TJ)
                    gate_up(b, par, t, first)
                    if t == WB_LAG:
                        weight_rows(b, first)
                    if t == 0:
                        if not first:
                            scores(b, 2)
                            scores(b, 3)
                            attend(b - 1, 1 - par, range(TJ))
                    if t == 2:
                        turn_weights(b)
                    if t == DOWN_LAG:
                        turn_probs(b, t - 3)
                    for h in due(t, DOWN_LAG, first, last, HOLD):
                        down(b, par, h)
                    if 3 <= t < DOWN_LAG:
                        turn_probs(b, t - 3)
                    if not last:
                        if t == 8:
                            pe.wait_ge(s_ptlo, b * TJ + 4)
                            turn_x(b + 1)
                        if t == 9:
                            keys_queries(b + 1, 1 - par)
                        if t == 10:
                            pe.wait_ge(s_klo, b + 2)
                            pe.wait_ge(s_qlo, b + 2)
                            values_logits(b + 1, 1 - par, att)

            bodies(pe, body)
            b, par = B - 1, (B - 1) % 2
            for s, t in enumerate(rest(DOWN_LAG)):
                attend(b, par, (s,))
                down(b, par, t)


_INS = ["x", "x_t", "front", "w_up", "w_down", "select"]


def kernel(**inputs):
    import numpy as _np
    import concourse.bacc as _bacc
    from concourse import mybir as _mybir
    from concourse.bass_utils import run_bass_kernel_spmd as _run

    a = {k.replace("L0_attn_", "").replace("L0_ffn_", "f_"): _np.asarray(v) for k, v in inputs.items()}
    f32 = _np.float32
    pad = _np.zeros((D, 1), f32)
    x_t = a["x"].reshape(B, P, TJ, D).transpose(0, 3, 2, 1).reshape(B, D, S)
    w_qkvr = _np.concatenate([a["Wq"], a["Wk"], a["Wv"], a["f_gate_w"].T, a["f_shared_expert_gate_w"].T, pad], axis=1)
    biases = _np.stack([a["bq"], a["bk"], a["bv"]], axis=1)
    gu = a["f_experts_gate_up"]

    def by_tile(m):
        return m.reshape(E, ET, PE_ROWS, -1).transpose(1, 0, 2, 3).reshape(E * I, -1)

    gate = _np.concatenate([by_tile(gu[:, :I]), a["f_shared_gate_w"]]).T
    up = _np.concatenate([by_tile(gu[:, I:]), a["f_shared_up_w"]]).T
    w_up = _np.concatenate([m[:, t * P:t * P + ROWS[t]] for t in range(NT) for m in (gate, up)], axis=1)
    w_up = w_up.reshape(P, CH, 2 * CW)
    down = _np.concatenate([by_tile(a["f_experts_down"].transpose(0, 2, 1)), a["f_shared_down_w"].T,
                            _np.zeros((NT * P - HID, D), f32)])
    w_down = down.reshape(NT, P, D).transpose(1, 0, 2).reshape(P, NT * D)
    tie = _np.zeros((E, E), f32)
    for e in range(E):
        tie[e, :e] = -1.2e-38
    front = _np.concatenate([w_qkvr, biases, _np.eye(P, dtype=f32), _np.tile(tie.reshape(1, E * E), (P, 1))], axis=1)
    select = _np.zeros((2 * R, 2 * P), f32)
    for p in range(P):
        e = p // PE_ROWS
        select[e, p] = select[R + e, p] = 1.0
    select[E, P:] = select[R + E, P:] = 1.0

    arrays = dict(zip(_INS, [a["x"], x_t, front, w_up, w_down, select]))
    nc = _bacc.Bacc("TRN2", target_bir_lowering=False, num_devices=1)
    feed, args = {}, []
    for name in _INS:
        m = _np.ascontiguousarray(arrays[name])
        feed[f"in_{name}_dram"] = m
        args.append(nc.dram_tensor(f"in_{name}_dram", m.shape, _mybir.dt.from_np(m.dtype), kind="ExternalInput").ap())
    out_t = nc.dram_tensor("out_t_dram", (B, D, S), F32, kind="ExternalOutput").ap()
    moe_attention_layer(nc, *args, out_t)
    y = _run(nc, [feed], core_ids=[0]).results[0]["out_t_dram"]
    return _np.ascontiguousarray(y.reshape(B, D, TJ, P).transpose(0, 3, 2, 1)).reshape(B, S, D)
```
